# Optimizing a Trainium2 kernel written in Bass

```python
import numpy as np
import jax
import jax.numpy as jnp

def _softmax(x, axis=-1):
    return jax.nn.softmax(x, axis=axis)

def _gelu(x):
    return jax.nn.gelu(x, approximate=True)

def _silu(x):
    return jax.nn.silu(x)

def _sigmoid(x):
    return jax.nn.sigmoid(x)

def _layernorm(x, axis=-1, eps=1e-05):
    m = jnp.mean(x, axis=axis, keepdims=True)
    v = jnp.var(x, axis=axis, keepdims=True)
    return (x - m) / jnp.sqrt(v + eps)

def _scatter_add(tgt, idx, src, axis=0):
    return tgt.at[idx].add(src)

def _segment_sum(src, seg, n):
    return jax.ops.segment_sum(src, seg, n)
kernel_name = 'mk_prb_d1_jaxref_r4_c44b06'

def setup_inputs(seed: int=0):
    np.random.seed(seed)
    _w = jnp.asarray

    def _L0_attn_setup():
        import jax, jax.numpy as jnp
        import numpy as np
        B, T, D = (4, 512, 256)
        H, Dh = (16, 64)
        key = jax.random.key(seed)
        ks = jax.random.split(key, 5)
        std_qkv = float(np.sqrt(2.0 / (Dh * D)))
        std_o = float(np.sqrt(2.0 / (D * Dh)))
        return {'x': jax.random.normal(ks[0], (B, T, D), dtype=jnp.float32), 'W_Q': jax.random.normal(ks[1], (H, Dh, D), dtype=jnp.float32) * std_qkv, 'b_Q': jnp.zeros((H, Dh), dtype=jnp.float32), 'W_K': jax.random.normal(ks[2], (H, Dh, D), dtype=jnp.float32) * std_qkv, 'b_K': jnp.zeros((H, Dh), dtype=jnp.float32), 'W_V': jax.random.normal(ks[3], (H, Dh, D), dtype=jnp.float32) * std_qkv, 'b_V': jnp.zeros((H, Dh), dtype=jnp.float32), 'W_O': jax.random.normal(ks[4], (H, D, Dh), dtype=jnp.float32) * std_o, 'b_O': jnp.zeros((D,), dtype=jnp.float32)}
    _L0_attn_in = _L0_attn_setup()

    def _L0_ffn_setup():
        import jax, jax.numpy as jnp
        import numpy as np
        E, K, H, I, SI = (32, 8, 256, 128, 512)
        CAP = 512
        LIMIT = 7.0
        SCALE = 2.5
        B, S = (2, 512)
        key = jax.random.key(seed)
        ks = jax.random.split(key, 8)
        s = 0.02
        return {'hidden_states': jax.random.normal(ks[0], (B, S, H), jnp.float32), 'router_weight': jax.random.normal(ks[1], (E, H), jnp.float32) * s, 'e_score_correction_bias': jnp.zeros((E,), jnp.float32), 'gate_up_proj': jax.random.normal(ks[2], (E, 2 * I, H), jnp.float32) * s, 'down_proj': jax.random.normal(ks[3], (E, H, I), jnp.float32) * s, 'shared_gate': jax.random.normal(ks[4], (SI, H), jnp.float32) * s, 'shared_up': jax.random.normal(ks[5], (SI, H), jnp.float32) * s, 'shared_down': jax.random.normal(ks[6], (H, SI), jnp.float32) * s}
    _L0_ffn_in = _L0_ffn_setup()
    _d = {'L0_attn_x': _L0_attn_in['x'], 'L0_attn_W_Q': _L0_attn_in['W_Q'], 'L0_attn_b_Q': _L0_attn_in['b_Q'], 'L0_attn_W_K': _L0_attn_in['W_K'], 'L0_attn_b_K': _L0_attn_in['b_K'], 'L0_attn_W_V': _L0_attn_in['W_V'], 'L0_attn_b_V': _L0_attn_in['b_V'], 'L0_attn_W_O': _L0_attn_in['W_O'], 'L0_attn_b_O': _L0_attn_in['b_O'], 'L0_ffn_router_weight': _L0_ffn_in['router_weight'], 'L0_ffn_e_score_correction_bias': _L0_ffn_in['e_score_correction_bias'], 'L0_ffn_gate_up_proj': _L0_ffn_in['gate_up_proj'], 'L0_ffn_down_proj': _L0_ffn_in['down_proj'], 'L0_ffn_shared_gate': _L0_ffn_in['shared_gate'], 'L0_ffn_shared_up': _L0_ffn_in['shared_up'], 'L0_ffn_shared_down': _L0_ffn_in['shared_down']}
    _x0 = _d['L0_attn_x']
    _d['L0_attn_x'] = jax.random.normal(jax.random.fold_in(jax.random.key(seed), 1), (2, 2048, 256), dtype=_x0.dtype)
    del _x0
    return _d

def reference(L0_attn_x, L0_attn_W_Q, L0_attn_b_Q, L0_attn_W_K, L0_attn_b_K, L0_attn_W_V, L0_attn_b_V, L0_attn_W_O, L0_attn_b_O, L0_ffn_router_weight, L0_ffn_e_score_correction_bias, L0_ffn_gate_up_proj, L0_ffn_down_proj, L0_ffn_shared_gate, L0_ffn_shared_up, L0_ffn_shared_down):

    def _L0_attn_ref(x, W_Q, b_Q, W_K, b_K, W_V, b_V, W_O, b_O):
        import jax, jax.numpy as jnp
        import numpy as np
        B, T, D = (4, 512, 256)
        H, Dh = (16, 64)
        Q = jnp.einsum('btd,hkd->bthk', x, W_Q) + b_Q
        K = jnp.einsum('btd,hkd->bthk', x, W_K) + b_K
        V = jnp.einsum('btd,hkd->bthk', x, W_V) + b_V
        d_head = W_Q.shape[1]
        scores = jnp.einsum('bqhk,bshk->bhqs', Q, K) / jnp.sqrt(jnp.asarray(d_head, x.dtype))
        attn = jax.nn.softmax(scores, axis=-1)
        out_h = jnp.einsum('bhqs,bshk->bqhk', attn, V)
        return jnp.einsum('bqhk,hdk->bqd', out_h, W_O) + b_O

    def _L0_ffn_ref(hidden_states, router_weight, e_score_correction_bias, gate_up_proj, down_proj, shared_gate, shared_up, shared_down):
        import jax, jax.numpy as jnp
        import numpy as np
        E, K, H, I, SI = (32, 8, 256, 128, 512)
        CAP = 512
        LIMIT = 7.0
        SCALE = 2.5
        B, S = (2, 512)
        b, s, _ = hidden_states.shape
        T = b * s
        x = hidden_states.reshape(T, H)
        logits = x.astype(jnp.float32) @ router_weight.astype(jnp.float32).T
        scores = jax.nn.sigmoid(logits)
        _, idx = jax.lax.top_k(scores + e_score_correction_bias, K)
        w = jnp.take_along_axis(scores, idx, axis=1)
        w = w / (w.sum(-1, keepdims=True) + 1e-20) * SCALE
        e_flat = idx.reshape(-1)
        onehot = jax.nn.one_hot(e_flat, E, dtype=jnp.int32)
        pos = jnp.cumsum(onehot, axis=0) - onehot
        pos = jnp.take_along_axis(pos, e_flat[:, None], axis=1)[:, 0]
        keep = pos < CAP
        slot = jnp.where(keep, e_flat * CAP + pos, E * CAP)
        tok = jnp.arange(T * K) // K
        buf = jnp.zeros((E * CAP + 1, H), x.dtype).at[slot].set(x[tok])
        xe = buf[:E * CAP].reshape(E, CAP, H)
        gu = jnp.einsum('ech,eoh->eco', xe, gate_up_proj)
        g, u = (gu[..., :I], gu[..., I:])
        g = jnp.minimum(g, LIMIT)
        u = jnp.clip(u, -LIMIT, LIMIT)
        h = jax.nn.silu(g) * u
        ye = jnp.einsum('eci,ehi->ech', h, down_proj)
        yp = ye.reshape(E * CAP, H)[jnp.minimum(slot, E * CAP - 1)]
        yp = jnp.where(keep[:, None], yp, 0.0) * w.reshape(-1)[:, None]
        routed = jax.ops.segment_sum(yp, tok, num_segments=T).reshape(b, s, H)
        shared = jax.nn.silu(hidden_states @ shared_gate.T) * (hidden_states @ shared_up.T) @ shared_down.T
        return routed + shared
    x = L0_attn_x
    xn = _layernorm(x, axis=-1)
    x = x + _L0_attn_ref(xn, L0_attn_W_Q, L0_attn_b_Q, L0_attn_W_K, L0_attn_b_K, L0_attn_W_V, L0_attn_b_V, L0_attn_W_O, L0_attn_b_O) + _L0_ffn_ref(xn, L0_ffn_router_weight, L0_ffn_e_score_correction_bias, L0_ffn_gate_up_proj, L0_ffn_down_proj, L0_ffn_shared_gate, L0_ffn_shared_up, L0_ffn_shared_down)
    return x

_drawn_inputs = setup_inputs


def setup_inputs(seed=0):
    import zlib

    import numpy as np

    out = dict(_drawn_inputs(seed))
    spreads = {'L0_attn_b_Q': (0.0, 2.0),
     'L0_attn_b_K': (0.0, 2.0),
     'L0_attn_b_V': (0.0, 2.0),
     'L0_attn_b_O': (0.0, 1.339),
     'L0_ffn_e_score_correction_bias': (0.0, 0.8)}
    factors = {'L0_attn_W_Q': 42.611,
     'L0_attn_W_K': 34.998,
     'L0_attn_W_V': 36.1,
     'L0_ffn_router_weight': 8.0,
     'L0_ffn_gate_up_proj': 8.0,
     'L0_ffn_down_proj': 8.0,
     'L0_ffn_shared_gate': 8.0,
     'L0_ffn_shared_up': 8.0,
     'L0_ffn_shared_down': 8.0}
    for name, (base, spread) in spreads.items():
        noise = np.random.default_rng([zlib.crc32(name.encode()), seed]).standard_normal(out[name].shape)
        drawn = base * np.exp(spread * noise) if base else spread * noise
        out[name] = jnp.asarray(drawn.astype(out[name].dtype))
    for name, factor in factors.items():
        out[name] = (out[name] * factor).astype(out[name].dtype)
    return out
```

```python
from contextlib import ExitStack

import concourse.bass as bass
from concourse import mybir

F32 = mybir.dt.float32
F32R = mybir.dt.float32r
BF16 = mybir.dt.bfloat16
U32 = mybir.dt.uint32
ALU = mybir.AluOpType
ACT = mybir.ActivationFunctionType
AX = mybir.AxisListType

P = 128
B, T, D = 2, 2048, 256
TOK = B * T
NT = TOK // P
DK = D // P
H, DH = 16, 64
E, K = 32, 8
I, SI = 128, 512
CAP = 512
LIMIT, SCALE, EPS = 7.0, 2.5, 1e-5
CH = 512
NC = TOK // CH
TPC = CH // P
NS = T // P
SLOTS = E * CAP


def wait_pos(eng, sem, value):
    if not isinstance(value, int) or value > 0:
        eng.wait_ge(sem, value)


def wait_apart(eng, sem, value, passed):
    if isinstance(value, int):
        wait_pos(eng, sem, value)
    else:
        eng.wait_ge(sem, value)
        eng.sem_inc(passed, 1)


class Memory:

    def __init__(self, nc, stack, tag):
        self.nc, self.stack, self.tag = nc, stack, tag

    def sb(self, name, shape, dt=F32):
        return self.stack.enter_context(self.nc.sbuf_tensor(f"{self.tag}_{name}", shape, dt))

    def ps(self, name, shape, dt=F32):
        return self.stack.enter_context(self.nc.psum_tensor(f"{self.tag}_{name}", shape, dt))

    def sem(self, name):
        return self.stack.enter_context(self.nc.semaphore(f"{self.tag}_{name}"))

    def sems(self, name, n):
        return [self.sem(f"{name}{i}") for i in range(n)]




def project_and_route(nc, io, scr, keep):
    with ExitStack() as stack:
        m = Memory(nc, stack, "pr")
        ps = m.ps("ps", [P, 8, CH])

        x_sb = m.sb("x", [P, NT, D])
        xn = m.sb("xn", [P, NT, D])
        xnT = m.sb("xnT", [P, DK, TOK])
        wq = m.sb("wq", [P, DK, H * DH])
        wk = m.sb("wk", [P, DK, H * DH])
        wv = m.sb("wv", [P, DK, H * DH])
        wg = m.sb("wg", [P, DK, SI])
        wu = m.sb("wu", [P, DK, SI])
        wd = m.sb("wd", [P, SI // P, D])
        wr = m.sb("wr", [P, DK, E])
        bq = m.sb("bq", [P, H // 2])
        bk = m.sb("bk", [P, H // 2])
        bv = m.sb("bv", [P, H * DH])
        bo = m.sb("bo", [P, D])
        eb = m.sb("eb", [P, E])

        stats = m.sb("stats", [P, NT, 6])
        moments = m.sb("moments", [P, NT, 2])
        veps = m.sb("veps", [P, NT])
        minus_half = m.sb("minus_half", [P, NT])
        rstd = m.sb("rstd", [P, NT])

        score = m.sb("score", [P, NT, E])
        mask = m.sb("mask", [P, NT, E])
        weight = m.sb("weight", [P, NT, E])
        key = m.sb("key", [P, NT, E])
        ebase = m.sb("ebase", [P, NT, E])
        tables = m.sb("tables", [P, 2, NT, E])
        ta, tb = tables[:, 0, :, :], tables[:, 1, :, :]
        maskb = m.sb("maskb", [P, NT * E], BF16)
        top = m.sb("top", [P, NT, K])
        wsum = m.sb("wsum", [P, NT])
        earlier = m.sb("earlier", [P, P], BF16)
        onesb = m.sb("onesb", [P, P], BF16)

        zeros = m.sb("zeros", [P, 4 * D])
        stage_x = m.sb("stage_x", [P, 2, D])
        stage_i = m.sb("stage_i", [P, 2, K], U32)
        part_hi = m.sb("part_hi", [P, 4, CH], F32R)
        part_lo = m.sb("part_lo", [P, 4, CH], F32R)
        v_sum = m.sb("v_sum", [P, 2, 512])
        v_parts = m.sb("v_parts", [P, 2, 8, 2, DH], F32R)
        silu_g = score[:, :, :].rearrange("p t e -> p (t e)").rearrange("p (u c) -> p u c", c=CH)
        hid = tables[:, :, :, :].rearrange("p a t e -> p (a t e)").rearrange("p (u c) -> p u c", c=CH)
        base = key[:, :, :].rearrange("p t e -> p (t e)").rearrange("p (t d) -> p t d", d=D)

        x_loaded = m.sems("x_loaded", 4)
        weights_loaded = m.sem("weights_loaded")
        zero_made = m.sem("zero_made")
        zero_stored = m.sem("zero_stored")
        consts_made = m.sem("consts_made")
        stats_done = m.sem("stats_done")
        moments_done = m.sem("moments_done")
        pool_step = m.sem("pool_step")
        rstd_done = m.sem("rstd_done")
        xn_done = m.sem("xn_done")
        xt_ready = m.sem("xt_ready")
        xnT_done = m.sem("xnT_done")
        logits_done = m.sem("logits_done")
        score_done = m.sem("score_done")
        mask_done = m.sem("mask_done")
        counts_done = m.sem("counts_done")
        counts_read = m.sem("counts_read")
        index_done = m.sem("index_done")
        route_step = m.sem("route_step")
        staged = m.sem("staged")
        scattered = m.sems("scattered", 2)
        qk_ready = m.sem("qk_ready")
        qk_hi = m.sem("qk_hi")
        qk_lo = m.sem("qk_lo")
        qk_stored = m.sems("qk_stored", 4)
        v_ready = m.sem("v_ready")
        v_summed = m.sem("v_summed")
        v_hi = m.sem("v_hi")
        v_lo = m.sem("v_lo")
        v_stored = m.sems("v_stored", 2)
        gu_ready = m.sem("gu_ready")
        silu_done = m.sem("silu_done")
        hid_done = m.sem("hid_done")
        down_ready = m.sem("down_ready")
        base_done = m.sem("base_done")
        base_stored = m.sem("base_stored")

        sp_waits, pool_waits = m.sem("sp_waits"), m.sem("pool_waits")
        block = stack.enter_context(nc.Block())
        XG = NT // 4
        ZR = SLOTS // P // 4
        N_WEIGHTS = 12

        def qk_units(c):
            for u in range(H):
                yield c * H + u, u, u % 2, u // 2

        @block.sync
        def _(sp):
            for g in range(4):
                sp.dma_start(x_sb[:, g * XG:(g + 1) * XG, :],
                             io["x"][g * XG * P:(g + 1) * XG * P, :].rearrange("(t p) d -> p t d", p=P)
                             ).then_inc(x_loaded[g], 16)
            for dst, src in ((wr, io["wr"]), (wq, io["wq"]), (wk, io["wk"]), (wv, io["wv"]), (wg, io["wg"]),
                             (wu, io["wu"]), (wd, io["wd"])):
                sp.dma_start(dst[:, :, :], src).then_inc(weights_loaded, 16)
            sp.dma_start(bq[:, :], io["bq"]).then_inc(weights_loaded, 16)
            sp.dma_start(bk[:, :], io["bk"]).then_inc(weights_loaded, 16)
            sp.dma_start(bv[:, :], io["bv"].partition_broadcast(P)).then_inc(weights_loaded, 16)
            sp.dma_start(bo[:, :], io["bo"].partition_broadcast(P)).then_inc(weights_loaded, 16)
            sp.dma_start(eb[:, :], io["eb"].partition_broadcast(P)).then_inc(weights_loaded, 16)
            sp.wait_ge(zero_made, 1)
            for g in range(ZR):
                sp.dma_start(scr["xbuf"].rearrange("(g p r) d -> g p (r d)", p=P, r=4)[g], zeros[:, :]
                             ).then_inc(zero_stored, 16)
            sp.dma_start(scr["ye"][SLOTS:SLOTS + P, :], zeros[:, 0:D]).then_inc(zero_stored, 16)

            def store_qk(c):
                for n, u, is_key, pair in qk_units(c):
                    dst = scr["k" if is_key else "q"]
                    wait_apart(sp, qk_lo, n + 1, sp_waits)
                    for part, src in ((0, part_hi), (1, part_lo)):
                        sp.dma_start(dst[part, pair * P:(pair + 1) * P, bass.ds(c * CH, CH)],
                                     src[:, u % 4, :].bitcast(F32)).then_inc(qk_stored[u % 4], 16)

            with sp.Fori(0, NC) as c:
                store_qk(c)
            for t in range(NT):
                for half in range(2):
                    n = 2 * t + half
                    wait_apart(sp, v_lo, n + 1, sp_waits)
                    sp.dma_start(scr["v"][half * 8:half * 8 + 8, :, t, :].rearrange("h p c -> p h c"),
                                 v_parts[:, half, :, :, :].rearrange("p h a c -> p h (a c)").bitcast(F32)
                                 ).then_inc(v_stored[half], 16)
            with sp.Fori(0, NC) as c:
                wait_apart(sp, base_done, c + 1, sp_waits)
                sp.dma_start(scr["base"][:, bass.ds(c * TPC, TPC), :], base[:, :, :]).then_inc(base_stored, 16)
            for n in range(4):
                sp.wait_ge(qk_stored[n], NC * H // 4 * 32)
            for half in range(2):
                sp.wait_ge(v_stored[half], NT * 16)
            sp.wait_ge(base_stored, NC * 16)
            sp.wait_ge(zero_stored, (ZR + 1) * 16)

        @block.gpsimd
        def _(pool):
            ident, n = keep["ident"], 0
            nc.gpsimd.memset(ident[:, :], 0.0)
            nc.gpsimd.memset(earlier[:, :], 1.0)
            nc.gpsimd.memset(onesb[:, :], 1.0)
            nc.gpsimd.memset(minus_half[:, :], -0.5).then_inc(pool_step, 1)
            pool.wait_ge(pool_step, 1)
            nc.gpsimd.affine_select(out=ident[:, :], in_=ident[:, :], compare_op=ALU.not_equal, fill=1.0,
                                    base=0, pattern=[[-1, P]], channel_multiplier=1)
            nc.gpsimd.affine_select(out=earlier[:, :], in_=earlier[:, :], compare_op=ALU.is_gt, fill=0.0,
                                    base=0, pattern=[[1, P]], channel_multiplier=-1)
            nc.gpsimd.iota(ebase[:, :, :], pattern=[[0, NT], [CAP, E]], base=1, channel_multiplier=0,
                           allow_small_or_imprecise_dtypes=True).then_inc(consts_made, 1)
            for g in range(4):
                tiles = slice(g * XG, (g + 1) * XG)
                wait_apart(pool, moments_done, g + 1, pool_waits)
                nc.gpsimd.tensor_scalar(veps[:, tiles], moments[:, tiles, 1], EPS, None, ALU.add
                                        ).then_inc(pool_step, 1)
                wait_apart(pool, pool_step, g + 2, pool_waits)
                nc.gpsimd.tensor_tensor(rstd[:, tiles], veps[:, tiles], minus_half[:, tiles], ALU.pow
                                        ).then_inc(rstd_done, 1)
            pool.wait_ge(index_done, 1)
            pool.wait_ge(zero_stored, (ZR + 1) * 16)

            def scatter(i):
                for q in range(2):
                    wait_apart(pool, scattered[q], i * (K * 16), pool_waits)
                    nc.gpsimd.tensor_copy(stage_i[:, q, :], keep["index"][:, bass.ds(2 * i + q, 1), :]
                                          .rearrange("p a k -> p (a k)"))
                    nc.gpsimd.tensor_copy(stage_x[:, q, :], xn[:, bass.ds(2 * i + q, 1), :]
                                          .rearrange("p a d -> p (a d)")).then_inc(staged, 1)
                    wait_apart(pool, staged, 2 * i + q + 1, pool_waits)
                    for k in range(K):
                        nc.gpsimd.indirect_dma_start(
                            out=scr["xbuf"][:, :],
                            out_offset=bass.IndirectOffsetOnAxis(ap=stage_i[:, q, k:k + 1], axis=0),
                            in_=stage_x[:, q, :], in_offset=None,
                            bounds_check=SLOTS - 1, oob_is_err=False).then_inc(scattered[q], 16)
            scatter(0)
            with pool.Fori(1, NT // 2) as i:
                scatter(i)
            for q in range(2):
                pool.wait_ge(scattered[q], NT // 2 * K * 16)

        @block.scalar
        def _(act):
            for n in range(2 * NC):
                act.wait_ge(xt_ready, n + 1)
                nc.scalar.copy(xnT[:, n % 2, (n // 2) * CH:(n // 2 + 1) * CH], ps[:, n % 4, :]
                               ).then_inc(xnT_done, 1)
            for half in range(2):
                act.wait_ge(logits_done, half + 1)
                nc.scalar.activation(score[:, half * 16:half * 16 + 16, :],
                                     ps[:, 4 + half, :].rearrange("p (t e) -> p t e", e=E), ACT.Sigmoid
                                     ).then_inc(score_done, 1)

            def qk_high(c):
                for n, u, is_key, pair in qk_units(c):
                    bias = (bk if is_key else bq)[:, pair:pair + 1]
                    act.wait_ge(qk_ready, n + 1)
                    wait_pos(act, qk_stored[u % 4], (c * 4 + u // 4) * 32)
                    nc.scalar.activation(part_hi[:, u % 4, :], ps[:, 4 + u % 4, :], ACT.Identity, bias=bias
                                         ).then_inc(qk_hi, 1)

            qk_high(0)
            with act.Fori(1, NC) as c:
                qk_high(c)
            for n in range(2 * NT):
                act.wait_ge(v_summed, n + 1)
                wait_pos(act, v_stored[n % 2], (n // 2) * 16)
                nc.scalar.copy(v_parts[:, n % 2, :, 0, :],
                               v_sum[:, n % 2, :].rearrange("p (h c) -> p h c", c=DH)).then_inc(v_hi, 1)
            with act.Fori(0, NC) as c:
                for u in range(4):
                    act.wait_ge(gu_ready, c * 4 + u + 1)
                    nc.scalar.activation(silu_g[:, u % 2, :], ps[:, 2 * (u % 2), :], ACT.Silu
                                         ).then_inc(silu_done, 1)

        @block.vector
        def _(dve):
            nc.vector.memset(zeros[:, :], 0.0).then_inc(zero_made, 1)
            for g in range(4):
                tiles = range(g * XG, (g + 1) * XG)
                dve.wait_ge(x_loaded[g], 16)
                for t in tiles:
                    last = nc.vector.bn_stats(stats[:, t, :], x_sb[:, t, :])
                last.then_inc(stats_done, 1)
                dve.wait_ge(stats_done, g + 1)
                for t in tiles:
                    last = nc.vector.bn_aggr(moments[:, t, :], stats[:, t, :])
                last.then_inc(moments_done, 1)
                dve.wait_ge(moments_done, g + 1)
                dve.wait_ge(rstd_done, g + 1)
                for t in tiles:
                    last = nc.vector.tensor_scalar(xn[:, t, :], x_sb[:, t, :], moments[:, t, 0:1],
                                                   rstd[:, t:t + 1], ALU.subtract, ALU.mult)
                    if t % TPC == TPC - 1:
                        last.then_inc(xn_done, 1)

            steps = [0]

            def link(ins):
                steps[0] += 1
                ins.then_inc(route_step, 1)
                dve.wait_ge(route_step, steps[0])

            dve.wait_ge(score_done, 2)
            dve.wait_ge(weights_loaded, N_WEIGHTS * 16)
            link(nc.vector.tensor_tensor(key[:, :, :], score[:, :, :],
                                         eb[:, :].unsqueeze(1).to_broadcast([P, NT, E]), ALU.add))
            for t in range(NT):
                last = nc.vector.max(top[:, t, :], key[:, t, :])
            link(last)
            for t in range(NT):
                last = nc.vector.match_replace(ta[:, t, :], top[:, t, :], key[:, t, :], -3.0e38)
            link(last)
            nc.vector.tensor_tensor(maskb[:, :].rearrange("p (t e) -> p t e", e=E), ta[:, :, :], key[:, :, :],
                                    ALU.not_equal).then_inc(mask_done, 1)
            link(nc.vector.tensor_tensor(mask[:, :, :], ta[:, :, :], key[:, :, :], ALU.not_equal))
            link(nc.vector.tensor_tensor(weight[:, :, :], score[:, :, :], mask[:, :, :], ALU.mult))
            link(nc.vector.tensor_reduce(wsum[:, :], weight[:, :, :], AX.X, ALU.add))
            link(nc.vector.tensor_scalar(wsum[:, :], wsum[:, :], 1e-20, None, ALU.add))
            link(nc.vector.reciprocal(wsum[:, :], wsum[:, :]))
            link(nc.vector.tensor_tensor(weight[:, :, :], weight[:, :, :],
                                         wsum[:, :].unsqueeze(2).to_broadcast([P, NT, E]), ALU.mult))
            nc.vector.tensor_scalar(weight[:, :, :], weight[:, :, :], SCALE, None, ALU.mult)
            dve.wait_ge(counts_done, 1)
            counts = ps[:, 2:4, :].rearrange("p b (t e) -> p (b t) e", e=E)
            within = ps[:, 0:2, :].rearrange("p b (t e) -> p (b t) e", e=E)
            link(nc.vector.tensor_copy(ta[:, :, :], counts))
            a, b = ta, tb
            for s in (1, 2, 4, 8, 16):
                nc.vector.tensor_copy(b[:, 0:s, :], a[:, 0:s, :])
                link(nc.vector.tensor_tensor(b[:, s:NT, :], a[:, s:NT, :], a[:, 0:NT - s, :], ALU.add))
                a, b = b, a
            link(nc.vector.tensor_tensor(b[:, :, :], counts, a[:, :, :], ALU.subtract))
            nc.vector.tensor_tensor(a[:, :, :], within, b[:, :, :], ALU.subtract).then_inc(counts_read, 1)
            dve.wait_ge(counts_read, 1)
            link(nc.vector.scalar_tensor_tensor(out=b[:, :, :], in0=a[:, :, :], scalar=float(CAP),
                                                in1=mask[:, :, :], op0=ALU.is_lt, op1=ALU.mult))
            dve.wait_ge(consts_made, 1)
            link(nc.vector.tensor_tensor(a[:, :, :], a[:, :, :], ebase[:, :, :], ALU.add))
            link(nc.vector.tensor_tensor(key[:, :, :], a[:, :, :], b[:, :, :], ALU.mult))
            for t in range(NT):
                last = nc.vector.max(top[:, t, :], key[:, t, :])
            link(last)
            rows = ta[:, 0:K, :].rearrange("p k e -> p (k e)")
            flat = top[:, :, :].rearrange("p t k -> p (t k)")
            link(nc.vector.tensor_scalar(rows, flat, 0.0, float(SLOTS + 1), ALU.is_equal, ALU.mult))
            nc.vector.scalar_tensor_tensor(out=keep["index"][:, :, :].rearrange("p t k -> p (t k)"), in0=rows,
                                           scalar=-1.0, in1=flat, op0=ALU.add, op1=ALU.add
                                           ).then_inc(index_done, 1)
            dve.wait_ge(index_done, 1)
            for k in range(K):
                link(nc.vector.tensor_tensor(ta[:, :, :], key[:, :, :],
                                             top[:, :, k:k + 1].to_broadcast([P, NT, E]), ALU.is_equal))
                link(nc.vector.tensor_tensor(tb[:, :, :], ta[:, :, :], weight[:, :, :], ALU.mult))
                nc.vector.tensor_reduce(keep["gain"][:, :, k:k + 1], tb[:, :, :], AX.X, ALU.add)
            link(nc.vector.tensor_tensor(x_sb[:, :, :], x_sb[:, :, :],
                                         bo[:, :].unsqueeze(1).to_broadcast([P, NT, D]), ALU.add))

            def qk_low(c):
                for n, u, is_key, pair in qk_units(c):
                    bias = (bk if is_key else bq)[:, pair:pair + 1]
                    dve.wait_ge(qk_hi, n + 1)
                    nc.vector.scalar_tensor_tensor(out=part_lo[:, u % 4, :], in0=ps[:, 4 + u % 4, :], scalar=bias,
                                                   in1=part_hi[:, u % 4, :].bitcast(F32), op0=ALU.add,
                                                   op1=ALU.subtract).then_inc(qk_lo, 1)

            with dve.Fori(0, NC) as c:
                qk_low(c)

            def v_low(n):
                dve.wait_ge(v_hi, n + 1)
                nc.vector.tensor_tensor(v_parts[:, n % 2, :, 1, :],
                                        v_sum[:, n % 2, :].rearrange("p (h c) -> p h c", c=DH),
                                        v_parts[:, n % 2, :, 0, :].bitcast(F32), ALU.subtract).then_inc(v_lo, 1)

            for n in range(2 * NT):
                dve.wait_ge(v_ready, n + 1)
                wait_pos(dve, v_lo, n - 1)
                nc.vector.tensor_tensor(v_sum[:, n % 2, :], ps[:, n % 4, :],
                                        bv[:, (n % 2) * 512:(n % 2 + 1) * 512], ALU.add).then_inc(v_summed, 1)
                if n:
                    v_low(n - 1)
            v_low(2 * NT - 1)

            def shared(c):
                for u in range(4):
                    dve.wait_ge(silu_done, c * 4 + u + 1)
                    if u == 0:
                        wait_pos(dve, down_ready, c)
                    nc.vector.tensor_tensor(hid[:, u, :], silu_g[:, u % 2, :], ps[:, 2 * (u % 2) + 1, :],
                                            ALU.mult).then_inc(hid_done, 1)
                dve.wait_ge(down_ready, c + 1)
                wait_pos(dve, base_stored, c * 16)
                for h in range(2):
                    last = nc.vector.tensor_tensor(base[:, 2 * h:2 * h + 2, :],
                                                   ps[:, 4 + h, :].rearrange("p (t d) -> p t d", d=D),
                                                   x_sb[:, bass.ds(c * TPC + 2 * h, 2), :], ALU.add)
                last.then_inc(base_done, 1)

            shared(0)
            with dve.Fori(1, NC) as c:
                shared(c)

        @block.tensor
        def _(pe):
            def logits(c):
                pe.wait_ge(xnT_done, 2 * c + 2)
                for t in range(c * TPC, (c + 1) * TPC):
                    out = ps[:, 4 + t // 16, (t % 16) * E:(t % 16 + 1) * E]
                    for k in range(DK):
                        last = nc.tensor.matmul(out, xnT[:, k, t * P:(t + 1) * P], wr[:, k, :],
                                                start=(k == 0), stop=(k == DK - 1))
                    if t % 16 == 15:
                        last.then_inc(logits_done, 1)

            pe.wait_ge(consts_made, 1)
            for c in range(NC):
                pe.wait_ge(xn_done, c + 1)
                for k in range(DK):
                    n = 2 * c + k
                    wait_pos(pe, xnT_done, n - 3)
                    for j in range(TPC):
                        last = nc.tensor.transpose(ps[:, n % 4, j * P:(j + 1) * P],
                                                   xn[:, c * TPC + j, k * P:(k + 1) * P], keep["ident"][:, :])
                    last.then_inc(xt_ready, 1)
                if c == 0:
                    pe.wait_ge(weights_loaded, N_WEIGHTS * 16)
                if c:
                    logits(c - 1)
            logits(NC - 1)

            pe.wait_ge(mask_done, 1)
            for h in range(2):
                nc.tensor.matmul(ps[:, h, :], earlier[:, :], maskb[:, h * 512:(h + 1) * 512], start=True, stop=True)
                last = nc.tensor.matmul(ps[:, 2 + h, :], onesb[:, :], maskb[:, h * 512:(h + 1) * 512],
                                        start=True, stop=True)
            last.then_inc(counts_done, 1)

            def qk(c):
                for n, u, is_key, pair in qk_units(c):
                    w = wk if is_key else wq
                    wait_pos(pe, qk_lo, n - 3)
                    for k in range(DK):
                        last = nc.tensor.matmul(ps[:, 4 + u % 4, :], w[:, k, pair * P:(pair + 1) * P],
                                                xnT[:, k, bass.ds(c * CH, CH)],
                                                start=(k == 0), stop=(k == DK - 1))
                    last.then_inc(qk_ready, 1)

            qk(0)
            with pe.Fori(1, NC) as c:
                qk(c)
            pe.wait_ge(counts_read, 1)
            for n in range(2 * NT):
                t, half = n // 2, n % 2
                wait_pos(pe, v_summed, n - 3)
                for k in range(DK):
                    last = nc.tensor.matmul(ps[:, n % 4, :], xnT[:, k, t * P:(t + 1) * P],
                                            wv[:, k, half * 512:(half + 1) * 512],
                                            start=(k == 0), stop=(k == DK - 1))
                last.then_inc(v_ready, 1)

            def shared(c):
                for u in range(4):
                    wait_pos(pe, hid_done, c * 4 + u - 1)
                    for bank, w in ((2 * (u % 2), wg), (2 * (u % 2) + 1, wu)):
                        for k in range(DK):
                            last = nc.tensor.matmul(ps[:, bank, :], w[:, k, u * P:(u + 1) * P],
                                                    xnT[:, k, bass.ds(c * CH, CH)],
                                                    start=(k == 0), stop=(k == DK - 1))
                    last.then_inc(gu_ready, 1)
                pe.wait_ge(hid_done, c * 4 + 4)
                wait_pos(pe, base_done, c)
                for j in range(TPC):
                    for u in range(4):
                        last = nc.tensor.matmul(ps[:, 4 + j // 2, (j % 2) * D:(j % 2 + 1) * D],
                                                hid[:, u, j * P:(j + 1) * P], wd[:, u, :],
                                                start=(u == 0), stop=(u == 3))
                last.then_inc(down_ready, 1)

            pe.wait_ge(v_summed, 2 * NT)
            pe.wait_ge(qk_lo, NC * H)
            shared(0)
            with pe.Fori(1, NC) as c:
                shared(c)




def run_experts(nc, io, scr, keep):
    with ExitStack() as stack:
        m = Memory(nc, stack, "ex")
        ps = m.ps("ps", [P, 8, CH])
        CT = CAP // P
        xe = m.sb("xe", [P, 2, CT, D])
        xeT = m.sb("xeT", [P, 2, DK, CAP])
        gu = m.sb("gu", [P, 2, DK, 2 * I])
        dn = m.sb("dn", [P, 2, D])
        gate = m.sb("gate", [P, 2, CAP])
        up = m.sb("up", [P, 2, CAP])
        silu_g = m.sb("silu_g", [P, 2, CAP])
        hid = m.sb("hid", [P, 2, CAP])
        dn_old = m.sb("dn_old", [P, 2, D])
        ye = m.sb("ye", [P, 2, CT, D])

        loaded = m.sems("loaded", 2)
        turned = m.sem("turned")
        xeT_done = m.sem("xeT_done")
        gu_ready = m.sem("gu_ready")
        gate_done = m.sem("gate_done")
        up_done = m.sem("up_done")
        silu_done = m.sem("silu_done")
        hid_done = m.sem("hid_done")
        dn_kept = m.sem("dn_kept")
        down_ready = m.sem("down_ready")
        ye_done = m.sem("ye_done")
        stored = m.sems("stored", 2)
        sp_waits, pool_waits = m.sem("sp_waits"), m.sem("pool_waits")
        block = stack.enter_context(nc.Block())

        @block.sync
        def _(sp):
            def load(i):
                for q in range(2):
                    e = 2 * i + q
                    wait_apart(sp, turned, 2 * i + q - 1, sp_waits)
                    wait_apart(sp, gu_ready, 2 * i + q - 1, sp_waits)
                    wait_apart(sp, dn_kept, 2 * i + q - 1, sp_waits)
                    sp.dma_start(xe[:, q, :, :], scr["xbuf"][bass.ds(e * CAP, CAP), :]
                                 .rearrange("(t p) d -> p t d", p=P)).then_inc(loaded[q], 16)
                    sp.dma_start(gu[:, q, :, :], io["gu"][bass.ds(e, 1), :, :, :]
                                 .rearrange("a p k o -> p (a k) o")).then_inc(loaded[q], 16)
                    sp.dma_start(dn[:, q, :], io["dn"][bass.ds(e, 1), :, :]
                                 .rearrange("a p d -> p (a d)")).then_inc(loaded[q], 16)

            load(0)
            with sp.Fori(1, E // 2) as i:
                load(i)

        @block.gpsimd
        def _(pool):
            def store(i):
                for q in range(2):
                    e = 2 * i + q
                    wait_apart(pool, ye_done, 2 * i + q + 1, pool_waits)
                    pool.dma_start(scr["ye"][bass.ds(e * CAP, CAP), :].rearrange("(t p) d -> p t d", p=P),
                                   ye[:, q, :, :]).then_inc(stored[q], 16)

            with pool.Fori(0, E // 2) as i:
                store(i)
            for q in range(2):
                pool.wait_ge(stored[q], E // 2 * 16)

        @block.scalar
        def _(act):
            def turn(i, q):
                n = 2 * i + q
                act.wait_ge(turned, n + 1)
                nc.scalar.copy(xeT[:, q, :, :], ps[:, 2 * q:2 * q + 2, :]).then_inc(xeT_done, 1)

            def down(i, q):
                n = 2 * i + q
                act.wait_ge(down_ready, n + 1)
                wait_pos(act, stored[q], i * 16)
                nc.scalar.copy(ye[:, q, :, :].rearrange("p t d -> p (t d)"),
                               ps[:, 2 * q:2 * q + 2, :].rearrange("p b c -> p (b c)")).then_inc(ye_done, 1)

            def silu(i, q):
                n = 2 * i + q
                act.wait_ge(gate_done, n + 1)
                nc.scalar.activation(silu_g[:, q, :], gate[:, q, :], ACT.Silu).then_inc(silu_done, 1)

            for q in range(2):
                turn(0, q)
                silu(0, q)

            def both(i):
                for q in range(2):
                    turn(i, q)
                    down(i - 1, q)
                    silu(i, q)

            both(1)
            with act.Fori(2, E // 2) as i:
                both(i)
            for q in range(2):
                down(E // 2 - 1, q)

        @block.vector
        def _(dve):
            def hidden(i):
                for q in range(2):
                    n = 2 * i + q
                    dve.wait_ge(gu_ready, n + 1)
                    wait_pos(dve, down_ready, n - 1)
                    nc.vector.tensor_copy(dn_old[:, q, :], dn[:, q, :]).then_inc(dn_kept, 1)
                    nc.vector.tensor_scalar(gate[:, q, :], ps[:, 4 + 2 * q, :], LIMIT, None, ALU.min
                                            ).then_inc(gate_done, 1)
                    nc.vector.tensor_scalar(up[:, q, :], ps[:, 5 + 2 * q, :], LIMIT, -LIMIT, ALU.min, ALU.max
                                            ).then_inc(up_done, 1)
                    dve.wait_ge(up_done, n + 1)
                    dve.wait_ge(silu_done, n + 1)
                    nc.vector.tensor_tensor(hid[:, q, :], silu_g[:, q, :], up[:, q, :], ALU.mult
                                            ).then_inc(hid_done, 1)

            hidden(0)
            with dve.Fori(1, E // 2) as i:
                hidden(i)

        @block.tensor
        def _(pe):
            def turn(i, q):
                pe.wait_ge(loaded[q], i * 48 + 48)
                wait_pos(pe, ye_done, 2 * i + q - 3)
                for k in range(DK):
                    for t in range(CT):
                        last = nc.tensor.transpose(ps[:, 2 * q + k, t * P:(t + 1) * P],
                                                   xe[:, q, t, k * P:(k + 1) * P], keep["ident"][:, :])
                last.then_inc(turned, 1)

            def gate_up(i, q):
                n = 2 * i + q
                pe.wait_ge(xeT_done, n + 1)
                wait_pos(pe, up_done, n - 1)
                for side in range(2):
                    for k in range(DK):
                        last = nc.tensor.matmul(ps[:, 4 + 2 * q + side, :], gu[:, q, k, side * I:(side + 1) * I],
                                                xeT[:, q, k, :], start=(k == 0), stop=(k == DK - 1))
                last.then_inc(gu_ready, 1)

            def down(i, q):
                n = 2 * i + q
                pe.wait_ge(hid_done, n + 1)
                pe.wait_ge(dn_kept, n + 1)
                for t in range(CT):
                    last = nc.tensor.matmul(ps[:, 2 * q + t // 2, (t % 2) * D:(t % 2 + 1) * D],
                                            hid[:, q, t * P:(t + 1) * P], dn_old[:, q, :], start=True, stop=True)
                last.then_inc(down_ready, 1)

            for q in range(2):
                turn(0, q)
                gate_up(0, q)
            def both(i):
                for q in range(2):
                    turn(i, q)
                    pe.wait_ge(xeT_done, 2 * i + q + 1)
                    down(i - 1, q)
                    gate_up(i, q)

            both(1)
            with pe.Fori(2, E // 2) as i:
                both(i)
            for q in range(2):
                down(E // 2 - 1, q)



GT = 4
TILES = T // P
GROUPS = TILES // GT
PV_LAG = GT + 1
OUT_LAG = 2 * GT + 1
LAST = OUT_LAG + TILES


def attend(nc, io, scr, keep):
    with ExitStack() as stack:
        m = Memory(nc, stack, "at")
        ps = m.ps("ps", [P, 8, CH])
        q_hh = m.sb("q_hh", [P, 2, CH], F32R)
        q_ll = m.sb("q_ll", [P, 2, CH], F32R)
        k_hl = m.sb("k_hl", [P, 2, T], F32R)
        v_hl = m.sb("v_hl", [P, NS, P], F32R)
        wo = m.sb("wo", [P, 2, D])
        prob = m.sb("prob", [P, 2, T])
        pT_hi = m.sb("pT_hi", [P, 2, NS, CH], F32R)
        pT_lo = m.sb("pT_lo", [P, 2, NS, CH], F32R)
        oT = m.sb("oT", [P, 2, CH])
        acc = m.sb("acc", [P, TILES, D])
        half_max = m.sb("half_max", [P, 2, 2])
        neg_max = m.sb("neg_max", [P, 2])
        half_sum = m.sb("half_sum", [P, TILES, 2])
        total = m.sb("total", [P, TILES])
        inv = m.sb("inv", [P, TILES])

        g_index = m.sb("g_index", [P, K], U32)
        g_gain = m.sb("g_gain", [P, K])
        rows = m.sb("rows", [P, 4, D])
        rest = m.sb("rest", [P, D])
        rest_t = m.sb("rest_t", [P, D])

        q_loaded = m.sems("q_loaded", 2)
        k_loaded = m.sems("k_loaded", 2)
        v_loaded = m.sems("v_loaded", GT)
        wo_loaded = m.sems("wo_loaded", 2)
        scored = m.sem("scored")
        max_step = m.sem("max_step")
        max_done = m.sem("max_done")
        exp_done = m.sem("exp_done")
        turned = m.sem("turned")
        high_done = m.sem("high_done")
        low_done = m.sem("low_done")
        pv_done = m.sem("pv_done")
        oT_done = m.sem("oT_done")
        sum_step = m.sem("sum_step")
        inv_done = m.sem("inv_done")
        projected = m.sem("projected")
        cleared = m.sem("cleared")
        added = m.sem("added")
        rest_loaded = m.sem("rest_loaded")
        finished = m.sem("finished")
        stored = m.sem("stored")
        g_staged = m.sem("g_staged")
        g_base = m.sem("g_base")
        gathered = m.sem("gathered")
        g_step = m.sem("g_step")
        g_stored = m.sem("g_stored")
        sp_waits, pool_waits = m.sem("sp_waits"), m.sem("pool_waits")
        block = stack.enter_context(nc.Block())

        def slots(b, h):
            head = b * H + h
            whole = isinstance(h, int)
            for s in range(LAST if whole and h == H - 1 else TILES):
                tile = head * TILES + s
                back = [(s - 1) // GT, (s - PV_LAG) // GT, (s - OUT_LAG) // GT]
                turn = not (whole and h == 0) or s >= 1
                pv = not (whole and h == 0) or s >= PV_LAG
                out = not (whole and h == 0) or s >= OUT_LAG
                yield dict(
                    s=s, head=head, tile=tile, scores=s < TILES, turn=turn and s <= TILES,
                    pv=(head * GROUPS + back[1], back[1] % 2, (s - PV_LAG) % GT)
                    if pv and s < PV_LAG + TILES else None,
                    out=(head * GROUPS + back[2], back[2] % GROUPS, (s - OUT_LAG) % GT, s < OUT_LAG)
                    if out and s < OUT_LAG + TILES else None)

        def over_heads(eng, body):
            for b in range(B):
                for s in slots(b, 0):
                    body(b, 0, s)
                with eng.Fori(1, H - 1) as h:
                    for s in slots(b, h):
                        body(b, h, s)
                for s in slots(b, H - 1):
                    body(b, H - 1, s)

        @block.sync
        def _(sp):
            def load_q(b, h, g):
                group = (b * H + h) * GROUPS + g
                wait_apart(sp, scored, 2 * GT * (group - 1), sp_waits)
                for part, dst in ((0, q_hh), (1, q_ll)):
                    src = scr["q"][part, bass.ds(h * DH, DH), b * T + g * CH:b * T + (g + 1) * CH]
                    for rows_ in (slice(0, DH), slice(DH, P)):
                        sp.dma_start(dst[rows_, g % 2, :].bitcast(F32), src).then_inc(q_loaded[g % 2], 16)

            def load_k(b, h, side):
                head = b * H + h
                wait_apart(sp, scored, 2 * ((head - 1) * TILES + (side + 1) * TILES // 2), sp_waits)
                for part in range(2):
                    sp.dma_start(k_hl[part * DH:(part + 1) * DH, side, :].bitcast(F32),
                                 scr["k"][part, bass.ds(h * DH, DH), b * T:(b + 1) * T]).then_inc(k_loaded[side], 16)

            def load_v(b, h, quarter):
                wait_apart(sp, pv_done, GT * ((b * H + h) * GROUPS - 1) + quarter + 1, sp_waits)
                tiles = slice(quarter * GT, (quarter + 1) * GT)
                sp.dma_start(v_hl[:, tiles, :].bitcast(F32),
                             scr["v"][bass.ds(h, 1), :, b * NS + quarter * GT:b * NS + (quarter + 1) * GT, :]
                             .rearrange("a p t c -> p (a t) c")).then_inc(v_loaded[quarter], 16)

            def load_wo(b, h, side):
                wait_apart(sp, projected, (b * H + h) * TILES - TILES // 2 * (1 - side), sp_waits)
                sp.dma_start(wo[:, side, :], io["wo"][bass.ds(h, 1), :, :].rearrange("a p d -> p (a d)")
                             ).then_inc(wo_loaded[side], 16)

            def head_loads(b, h, following):
                load_q(b, h, 1)
                load_k(b, h, 1)
                load_wo(b, h, 0)
                for quarter in range(GT):
                    load_v(b, h, quarter)
                load_q(b, h, 2)
                load_q(b, h, 3)
                load_wo(b, h, 1)
                if following is not None:
                    load_k(*following, 0)
                    load_q(*following, 0)

            def finish_batch(b):
                for t in range(TILES):
                    n = b * TILES + t
                    wait_apart(sp, finished, n, sp_waits)
                    wait_apart(sp, g_stored, 16 * (n + 1), sp_waits)
                    sp.dma_start(rest_t[:, :], scr["rest"][:, n, :]).then_inc(rest_loaded, 16)
                    wait_apart(sp, finished, n + 1, sp_waits)
                    sp.dma_start(io["out"][n * P:(n + 1) * P, :], acc[:, t, :]).then_inc(stored, 16)

            load_k(0, 0, 0)
            load_q(0, 0, 0)
            for b in range(B):
                head_loads(b, 0, (b, 1))
                with sp.Fori(1, H - 1) as h:
                    head_loads(b, h, (b, h + 1))
                head_loads(b, H - 1, (b + 1, 0) if b + 1 < B else None)
                finish_batch(b)
            sp.wait_ge(stored, B * TILES * 16)

        @block.gpsimd
        def _(pool):
            def gather(n, k):
                nc.gpsimd.indirect_dma_start(
                    out=rows[:, k % 4, :], out_offset=None, in_=scr["ye"][:, :],
                    in_offset=bass.IndirectOffsetOnAxis(ap=g_index[:, k:k + 1], axis=0),
                    bounds_check=SLOTS, oob_is_err=True).then_inc(gathered, 16)

            with pool.Fori(0, NT) as n:
                nc.gpsimd.tensor_copy(g_index[:, :], keep["index"][:, bass.ds(n, 1), :]
                                      .rearrange("p a k -> p (a k)"))
                nc.gpsimd.tensor_copy(g_gain[:, :], keep["gain"][:, bass.ds(n, 1), :]
                                      .rearrange("p a k -> p (a k)")).then_inc(g_staged, 1)
                pool.dma_start(rest[:, :], scr["base"][:, bass.ds(n, 1), :].rearrange("p a d -> p (a d)")
                               ).then_inc(g_base, 16)
                wait_apart(pool, g_staged, n + 1, pool_waits)
                for r in range(2):
                    for k in range(4 * r, 4 * r + 4):
                        gather(n, k)
                    if r == 0:
                        wait_apart(pool, g_base, n * 16 + 16, pool_waits)
                    wait_apart(pool, gathered, n * (K * 16) + (r + 1) * 64, pool_waits)
                    for k in range(4):
                        nc.gpsimd.tensor_scalar(rows[:, k, :], rows[:, k, :], g_gain[:, 4 * r + k:4 * r + k + 1],
                                                None, ALU.mult).then_inc(g_step, 1)
                        wait_apart(pool, g_step, n * (2 * K) + 8 * r + 2 * k + 1, pool_waits)
                        nc.gpsimd.tensor_tensor(rest[:, :], rest[:, :], rows[:, k, :], ALU.add).then_inc(g_step, 1)
                        wait_apart(pool, g_step, n * (2 * K) + 8 * r + 2 * k + 2, pool_waits)
                pool.dma_start(scr["rest"][:, bass.ds(n, 1), :].rearrange("p a d -> p (a d)"), rest[:, :]
                               ).then_inc(g_stored, 16)
                wait_apart(pool, g_stored, n * 16 + 16, pool_waits)

        @block.tensor
        def _(pe):
            def transpose(s, unit):
                n = (s["tile"] - 1) * GT + unit
                if unit == 0:
                    pe.wait_ge(exp_done, 2 * s["tile"])
                wait_pos(pe, low_done, n - 1)
                for j in range(GT):
                    t = unit * GT + j
                    last = nc.tensor.transpose(ps[:, 4 + unit % 2, j * P:(j + 1) * P],
                                               prob[:, (s["s"] - 1) % 2, t * P:(t + 1) * P], keep["ident"][:, :])
                last.then_inc(turned, 1)

            def body(b, h, s):
                if s["scores"]:
                    i, head = s["s"], s["head"]
                    g, j, side = i // GT, i % GT, i // (TILES // 2)
                    if j == 0:
                        pe.wait_ge(q_loaded[g % 2], 64 * (head * 2 + g // 2) + 64)
                    if i % (TILES // 2) == 0:
                        pe.wait_ge(k_loaded[side], 32 * head + 32)
                    for c in range(GT):
                        if c % 2 == 0:
                            wait_pos(pe, exp_done, 2 * s["tile"] - 1 + c // 2)
                        for q, first in ((q_hh, True), (q_ll, False)):
                            last = nc.tensor.matmul(ps[:, c, :], q[:, g % 2, j * P:(j + 1) * P],
                                                    k_hl[:, side, c * CH:(c + 1) * CH],
                                                    start=first, stop=not first)
                        if c % 2 == 1:
                            last.then_inc(scored, 1)
                if s["turn"]:
                    transpose(s, 0)
                    transpose(s, 1)
                if s["pv"]:
                    group, parity, quarter = s["pv"]
                    pe.wait_ge(low_done, group * (GT * GT) + (GT - 1) * GT + quarter + 1)
                    pe.wait_ge(v_loaded[quarter],
                               16 * (s["head"] + (1 if s["s"] >= PV_LAG and s["s"] < TILES + PV_LAG else 0)))
                    if quarter == 0:
                        wait_pos(pe, oT_done, group)
                    for t in range(quarter * GT, (quarter + 1) * GT):
                        for part in (pT_hi, pT_lo):
                            last = nc.tensor.matmul(ps[:, 6, :], v_hl[:, t, :], part[:, parity, t, :],
                                                    start=(t == 0 and part is pT_hi),
                                                    stop=(t == NS - 1 and part is pT_lo))
                    last.then_inc(pv_done, 1)
                if s["turn"]:
                    transpose(s, 2)
                if s["out"]:
                    group, g, j, behind = s["out"]
                    n = group * GT + j
                    if j == 0:
                        pe.wait_ge(oT_done, group + 1)
                        pe.wait_ge(wo_loaded[g // 2], 16 * (s["head"] + (0 if behind else 1)))
                    wait_pos(pe, added, n)
                    nc.tensor.matmul(ps[:, 7, 0:D], oT[:, g % 2, j * P:(j + 1) * P], wo[:, g // 2, :],
                                     start=True, stop=True).then_inc(projected, 1)
                if s["turn"]:
                    transpose(s, 3)

            over_heads(pe, body)

        @block.scalar
        def _(act):
            def high(s, lag, unit):
                i = s["s"] - lag
                n = (s["tile"] - lag) * GT + unit
                act.wait_ge(turned, n + 1)
                nc.scalar.copy(pT_hi[:, i // GT % 2, unit * GT:(unit + 1) * GT, i % GT * P:(i % GT + 1) * P],
                               ps[:, 4 + unit % 2, :].rearrange("p (t c) -> p t c", c=P)).then_inc(high_done, 1)

            def body(b, h, s):
                i, tile = s["s"], s["tile"]
                first = isinstance(h, int) and h == 0
                if i <= TILES + 1 and not (first and i < 2):
                    high(s, 2, 2)
                    high(s, 2, 3)
                if s["turn"]:
                    high(s, 1, 0)
                    high(s, 1, 1)
                if s["scores"]:
                    act.wait_ge(max_done, tile + 1)
                    wait_pos(act, turned, GT * (tile - 1))
                    for half in range(2):
                        nc.scalar.activation(prob[:, i % 2, half * 1024:(half + 1) * 1024],
                                             ps[:, 2 * half:2 * half + 2, :].rearrange("p b c -> p (b c)"),
                                             ACT.Exp, bias=neg_max[:, i % 2:i % 2 + 1], scale=DH ** -0.5,
                                             accum_out=half_sum[:, i % TILES, half:half + 1]).then_inc(exp_done, 1)
                if s["pv"] and s["pv"][2] == GT - 1:
                    group, parity, _ = s["pv"]
                    act.wait_ge(pv_done, GT * (group + 1))
                    wait_pos(act, projected, GT * (group - 1))
                    nc.scalar.copy(oT[:, parity, :], ps[:, 6, :]).then_inc(oT_done, 1)

            over_heads(act, body)

        @block.vector
        def _(dve):
            def low(s, lag, unit):
                i = s["s"] - lag
                n = (s["tile"] - lag) * GT + unit
                dve.wait_ge(high_done, n + 1)
                where = (slice(None), i // GT % 2, slice(unit * GT, (unit + 1) * GT), slice(i % GT * P, (i % GT + 1) * P))
                nc.vector.tensor_tensor(pT_lo[where], ps[:, 4 + unit % 2, :].rearrange("p (t c) -> p t c", c=P),
                                        pT_hi[where].bitcast(F32), ALU.subtract).then_inc(low_done, 1)

            def body(b, h, s):
                i, tile, head = s["s"], s["tile"], s["head"]
                first = isinstance(h, int) and h == 0
                if first and i == 0:
                    wait_pos(dve, stored, 16 * b * TILES)
                    nc.vector.memset(acc[:, :, :], 0.0).then_inc(cleared, 1)
                if i <= TILES + 1 and not (first and i < 2):
                    low(s, 2, 2)
                    low(s, 2, 3)
                if s["scores"]:
                    for half in range(2):
                        dve.wait_ge(scored, 2 * tile + half + 1)
                        nc.vector.tensor_reduce(half_max[:, i % 2, half:half + 1], ps[:, 2 * half:2 * half + 2, :],
                                                AX.XY, ALU.max).then_inc(max_step, 1)
                    dve.wait_ge(max_step, 2 * tile + 2)
                    wait_pos(dve, exp_done, 2 * (tile - 1))
                    nc.vector.tensor_scalar(neg_max[:, i % 2:i % 2 + 1], half_max[:, i % 2, 0:1],
                                            half_max[:, i % 2, 1:2], -(DH ** -0.5), ALU.max, ALU.mult
                                            ).then_inc(max_done, 1)
                if s["turn"]:
                    low(s, 1, 0)
                    low(s, 1, 1)
                if s["pv"] and s["pv"][2] == 0:
                    group = s["pv"][0]
                    g = (s["s"] - PV_LAG) // GT % GROUPS
                    tiles = slice(g * GT, (g + 1) * GT)
                    dve.wait_ge(exp_done, 2 * GT * (group + 1))
                    nc.vector.tensor_tensor(total[:, tiles], half_sum[:, tiles, 0], half_sum[:, tiles, 1], ALU.add
                                            ).then_inc(sum_step, 1)
                    dve.wait_ge(sum_step, group + 1)
                    nc.vector.reciprocal(inv[:, tiles], total[:, tiles]).then_inc(inv_done, 1)
                if s["out"]:
                    group, g, j, behind = s["out"]
                    n, t = group * GT + j, g * GT + j
                    dve.wait_ge(projected, n + 1)
                    if j == 0:
                        dve.wait_ge(inv_done, group + 1)
                    if first and i == OUT_LAG:
                        dve.wait_ge(cleared, b + 1)
                    wait_pos(dve, added, n - TILES // 2 + 1)
                    nc.vector.scalar_tensor_tensor(out=acc[:, t, :], in0=ps[:, 7, 0:D], scalar=inv[:, t:t + 1],
                                                   in1=acc[:, t, :], op0=ALU.mult, op1=ALU.add
                                                   ).then_inc(added, 1)
                if isinstance(h, int) and h == H - 1 and i == LAST - 1:
                    dve.wait_ge(added, (b + 1) * H * TILES)
                    for t in range(TILES):
                        n = b * TILES + t
                        dve.wait_ge(rest_loaded, 16 * (n + 1))
                        nc.vector.tensor_tensor(acc[:, t, :], acc[:, t, :], rest_t[:, :], ALU.add
                                                ).then_inc(finished, 1)

            over_heads(dve, body)


def build(nc, io):
    scr = {
        "xbuf": nc.dram_tensor("xbuf", (SLOTS, D), F32, kind="Internal").ap(),
        "ye": nc.dram_tensor("ye", (SLOTS + P, D), F32, kind="Internal").ap(),
        "q": nc.dram_tensor("q_parts", (2, H * DH, TOK), F32, kind="Internal").ap(),
        "k": nc.dram_tensor("k_parts", (2, H * DH, TOK), F32, kind="Internal").ap(),
        "v": nc.dram_tensor("v_parts", (H, P, NT, P), F32, kind="Internal").ap(),
        "base": nc.dram_tensor("base", (P, NT, D), F32, kind="Internal").ap(),
        "rest": nc.dram_tensor("rest", (P, NT, D), F32, kind="Internal").ap(),
    }
    with ExitStack() as stack:
        m = Memory(nc, stack, "keep")
        keep = {
            "ident": m.sb("ident", [P, P]),
            "index": m.sb("index", [P, NT, K], U32),
            "gain": m.sb("gain", [P, NT, K]),
        }
        project_and_route(nc, io, scr, keep)
        run_experts(nc, io, scr, keep)
        attend(nc, io, scr, keep)


def kernel(**inputs):
    import numpy as np
    import concourse.bacc as bacc
    from concourse.bass_utils import run_bass_kernel_spmd

    a = {n: np.asarray(v) for n, v in inputs.items()}

    def halves(w):
        return w.T.reshape(DK, P, -1).transpose(1, 0, 2)

    wo = a["L0_attn_W_O"].transpose(0, 2, 1)
    gu = a["L0_ffn_gate_up_proj"].transpose(0, 2, 1).reshape(E, DK, P, 2 * I)
    laid = {
        "x": a["L0_attn_x"].reshape(TOK, D),
        "wq": halves(a["L0_attn_W_Q"].reshape(H * DH, D)),
        "wk": halves(a["L0_attn_W_K"].reshape(H * DH, D)),
        "wv": halves(a["L0_attn_W_V"].reshape(H * DH, D)),
        "bq": a["L0_attn_b_Q"].reshape(H // 2, P).T,
        "bk": a["L0_attn_b_K"].reshape(H // 2, P).T,
        "bv": a["L0_attn_b_V"].reshape(H * DH),
        "bo": a["L0_attn_b_O"],
        "wo": np.concatenate([wo, wo], axis=1),
        "wr": halves(a["L0_ffn_router_weight"]),
        "eb": a["L0_ffn_e_score_correction_bias"],
        "gu": gu.transpose(0, 2, 1, 3),
        "dn": a["L0_ffn_down_proj"].transpose(0, 2, 1),
        "wg": halves(a["L0_ffn_shared_gate"]),
        "wu": halves(a["L0_ffn_shared_up"]),
        "wd": a["L0_ffn_shared_down"].T.reshape(SI // P, P, D).transpose(1, 0, 2),
    }
    nc = bacc.Bacc("TRN2", target_bir_lowering=False, num_devices=1)
    arrays, io = {}, {}
    for name, v in laid.items():
        v = np.ascontiguousarray(v)
        arrays[f"in_{name}"] = v
        io[name] = nc.dram_tensor(f"in_{name}", v.shape, mybir.dt.from_np(v.dtype), kind="ExternalInput").ap()
    io["out"] = nc.dram_tensor("out", (TOK, D), F32, kind="ExternalOutput").ap()
    build(nc, io)
    r = run_bass_kernel_spmd(nc, [arrays], core_ids=[0])
    return r.results[0]["out"].reshape(B, T, D)
```

```python
from contextlib import ExitStack

import concourse.bass as bass
from concourse import mybir

F32 = mybir.dt.float32
F32R = mybir.dt.float32r
BF16 = mybir.dt.bfloat16
U32 = mybir.dt.uint32
ALU = mybir.AluOpType
ACT = mybir.ActivationFunctionType
AX = mybir.AxisListType

P = 128
B, T, D = 2, 2048, 256
TOK = B * T
NT = TOK // P
DK = D // P
H, DH = 16, 64
E, K = 32, 8
I, SI = 128, 512
CAP = 512
LIMIT, SCALE, EPS = 7.0, 2.5, 1e-5
CH = 512
NC = TOK // CH
TPC = CH // P
NS = T // P
SLOTS = E * CAP


def wait_pos(eng, sem, value):
    if not isinstance(value, int) or value > 0:
        eng.wait_ge(sem, value)


def wait_apart(eng, sem, value, passed):
    if isinstance(value, int):
        wait_pos(eng, sem, value)
    else:
        eng.wait_ge(sem, value)
        eng.sem_inc(passed, 1)


class Memory:

    def __init__(self, nc, stack, tag):
        self.nc, self.stack, self.tag = nc, stack, tag

    def sb(self, name, shape, dt=F32):
        return self.stack.enter_context(self.nc.sbuf_tensor(f"{self.tag}_{name}", shape, dt))

    def ps(self, name, shape, dt=F32):
        return self.stack.enter_context(self.nc.psum_tensor(f"{self.tag}_{name}", shape, dt))

    def sem(self, name):
        return self.stack.enter_context(self.nc.semaphore(f"{self.tag}_{name}"))

    def sems(self, name, n):
        return [self.sem(f"{name}{i}") for i in range(n)]




def project_and_route(nc, io, scr, keep):
    with ExitStack() as stack:
        m = Memory(nc, stack, "pr")
        ps = m.ps("ps", [P, 8, CH])

        x_sb = m.sb("x", [P, NT, D])
        xn = m.sb("xn", [P, NT, D])
        xnT = m.sb("xnT", [P, DK, TOK])
        wq = m.sb("wq", [P, DK, H * DH])
        wk = m.sb("wk", [P, DK, H * DH])
        wv = m.sb("wv", [P, DK, H * DH])
        wg = m.sb("wg", [P, DK, SI])
        wu = m.sb("wu", [P, DK, SI])
        wd = m.sb("wd", [P, SI // P, D])
        wr = m.sb("wr", [P, DK, E])
        bq = m.sb("bq", [P, H // 2])
        bk = m.sb("bk", [P, H // 2])
        bv = m.sb("bv", [P, H * DH])
        bo = m.sb("bo", [P, D])
        eb = m.sb("eb", [P, E])

        stats = m.sb("stats", [P, NT, 6])
        moments = m.sb("moments", [P, NT, 2])
        veps = m.sb("veps", [P, NT])
        minus_half = m.sb("minus_half", [P, NT])
        rstd = m.sb("rstd", [P, NT])

        score = m.sb("score", [P, NT, E])
        mask = m.sb("mask", [P, NT, E])
        weight = m.sb("weight", [P, NT, E])
        key = m.sb("key", [P, NT, E])
        ebase = m.sb("ebase", [P, NT, E])
        tables = m.sb("tables", [P, 2, NT, E])
        ta, tb = tables[:, 0, :, :], tables[:, 1, :, :]
        maskb = m.sb("maskb", [P, NT * E], BF16)
        top = m.sb("top", [P, NT, K])
        wsum = m.sb("wsum", [P, NT])
        earlier = m.sb("earlier", [P, P], BF16)
        onesb = m.sb("onesb", [P, P], BF16)

        zeros = m.sb("zeros", [P, 4 * D])
        stage_x = m.sb("stage_x", [P, 2, D])
        stage_i = m.sb("stage_i", [P, 2, K], U32)
        part_hi = m.sb("part_hi", [P, 4, CH], F32R)
        part_lo = m.sb("part_lo", [P, 4, CH], F32R)
        v_sum = m.sb("v_sum", [P, 2, 512])
        v_parts = m.sb("v_parts", [P, 2, 8, 2, DH], F32R)
        silu_g = score[:, :, :].rearrange("p t e -> p (t e)").rearrange("p (u c) -> p u c", c=CH)
        hid = tables[:, :, :, :].rearrange("p a t e -> p (a t e)").rearrange("p (u c) -> p u c", c=CH)
        base = key[:, :, :].rearrange("p t e -> p (t e)").rearrange("p (t d) -> p t d", d=D)

        x_loaded = m.sems("x_loaded", 4)
        wr_loaded = m.sem("wr_loaded")
        weights_loaded = m.sem("weights_loaded")
        zero_made = m.sem("zero_made")
        zero_stored = m.sem("zero_stored")
        consts_made = m.sem("consts_made")
        stats_done = m.sem("stats_done")
        moments_done = m.sem("moments_done")
        pool_step = m.sem("pool_step")
        rstd_done = m.sem("rstd_done")
        xn_done = m.sem("xn_done")
        xt_ready = m.sem("xt_ready")
        xnT_done = m.sem("xnT_done")
        logits_done = m.sem("logits_done")
        score_done = m.sem("score_done")
        mask_done = m.sem("mask_done")
        counts_done = m.sem("counts_done")
        counts_read = m.sem("counts_read")
        index_done = m.sem("index_done")
        route_step = m.sem("route_step")
        staged = m.sem("staged")
        scattered = m.sems("scattered", 2)
        qk_ready = m.sem("qk_ready")
        qk_hi = m.sem("qk_hi")
        qk_lo = m.sem("qk_lo")
        qk_sum = m.sem("qk_sum")
        qk_stored = m.sems("qk_stored", 4)
        v_ready = m.sem("v_ready")
        v_summed = m.sem("v_summed")
        v_hi = m.sem("v_hi")
        v_lo = m.sem("v_lo")
        v_stored = m.sems("v_stored", 2)
        gu_ready = m.sem("gu_ready")
        silu_done = m.sem("silu_done")
        hid_done = m.sem("hid_done")
        down_ready = m.sem("down_ready")
        base_done = m.sem("base_done")
        base_stored = m.sem("base_stored")

        sp_waits, pool_waits = m.sem("sp_waits"), m.sem("pool_waits")
        block = stack.enter_context(nc.Block())
        XG = NT // 4
        ZR = SLOTS // P // 4
        N_WEIGHTS = 11
        ROUTED = 2
        COUNTS_AT = 7

        def qk_units(c):
            for u in range(H):
                yield c * H + u, u, u % 2, u // 2

        @block.sync
        def _(sp):
            sp.dma_start(wr[:, :, :], io["wr"]).then_inc(wr_loaded, 16)
            for g in range(4):
                sp.dma_start(x_sb[:, g * XG:(g + 1) * XG, :],
                             io["x"][g * XG * P:(g + 1) * XG * P, :].rearrange("(t p) d -> p t d", p=P)
                             ).then_inc(x_loaded[g], 16)
            for dst, src in ((wq, io["wq"]), (wk, io["wk"]), (wv, io["wv"]), (wg, io["wg"]),
                             (wu, io["wu"]), (wd, io["wd"])):
                sp.dma_start(dst[:, :, :], src).then_inc(weights_loaded, 16)
            sp.dma_start(bq[:, :], io["bq"]).then_inc(weights_loaded, 16)
            sp.dma_start(bk[:, :], io["bk"]).then_inc(weights_loaded, 16)
            sp.dma_start(bv[:, :], io["bv"].partition_broadcast(P)).then_inc(weights_loaded, 16)
            sp.dma_start(bo[:, :], io["bo"].partition_broadcast(P)).then_inc(weights_loaded, 16)
            sp.dma_start(eb[:, :], io["eb"].partition_broadcast(P)).then_inc(weights_loaded, 16)
            sp.wait_ge(zero_made, 1)
            for g in range(ZR):
                sp.dma_start(scr["xbuf"].rearrange("(g p r) d -> g p (r d)", p=P, r=4)[g], zeros[:, :]
                             ).then_inc(zero_stored, 16)
            sp.dma_start(scr["ye"][SLOTS:SLOTS + P, :], zeros[:, 0:D]).then_inc(zero_stored, 16)

            def store_qk(c):
                for n, u, is_key, pair in qk_units(c):
                    dst = scr["k" if is_key else "q"]
                    wait_apart(sp, qk_lo, n + 1, sp_waits)
                    for part, src in ((0, part_hi), (1, part_lo)):
                        sp.dma_start(dst[part, pair * P:(pair + 1) * P, bass.ds(c * CH, CH)],
                                     src[:, u % 4, :].bitcast(F32)).then_inc(qk_stored[u % 4], 16)

            with sp.Fori(0, NC) as c:
                store_qk(c)
            for t in range(NT):
                for half in range(2):
                    n = 2 * t + half
                    wait_apart(sp, v_lo, n + 1, sp_waits)
                    sp.dma_start(scr["v"][half * 8:half * 8 + 8, :, t, :].rearrange("h p c -> p h c"),
                                 v_parts[:, half, :, :, :].rearrange("p h a c -> p h (a c)").bitcast(F32)
                                 ).then_inc(v_stored[half], 16)
            with sp.Fori(0, NC) as c:
                wait_apart(sp, base_done, c + 1, sp_waits)
                sp.dma_start(scr["base"][:, bass.ds(c * TPC, TPC), :], base[:, :, :]).then_inc(base_stored, 16)
            for n in range(4):
                sp.wait_ge(qk_stored[n], NC * H // 4 * 32)
            for half in range(2):
                sp.wait_ge(v_stored[half], NT * 16)
            sp.wait_ge(base_stored, NC * 16)
            sp.wait_ge(zero_stored, (ZR + 1) * 16)

        @block.gpsimd
        def _(pool):
            ident, n = keep["ident"], 0
            nc.gpsimd.memset(ident[:, :], 0.0)
            nc.gpsimd.memset(earlier[:, :], 1.0)
            nc.gpsimd.memset(onesb[:, :], 1.0)
            nc.gpsimd.memset(minus_half[:, :], -0.5).then_inc(pool_step, 1)
            pool.wait_ge(pool_step, 1)
            nc.gpsimd.affine_select(out=ident[:, :], in_=ident[:, :], compare_op=ALU.not_equal, fill=1.0,
                                    base=0, pattern=[[-1, P]], channel_multiplier=1)
            nc.gpsimd.affine_select(out=earlier[:, :], in_=earlier[:, :], compare_op=ALU.is_gt, fill=0.0,
                                    base=0, pattern=[[1, P]], channel_multiplier=-1)
            nc.gpsimd.iota(ebase[:, :, :], pattern=[[0, NT], [CAP, E]], base=1, channel_multiplier=0,
                           allow_small_or_imprecise_dtypes=True).then_inc(consts_made, 1)
            for g in range(4):
                tiles = slice(g * XG, (g + 1) * XG)
                wait_apart(pool, moments_done, g + 1, pool_waits)
                nc.gpsimd.tensor_scalar(veps[:, tiles], moments[:, tiles, 1], EPS, None, ALU.add
                                        ).then_inc(pool_step, 1)
                wait_apart(pool, pool_step, g + 2, pool_waits)
                nc.gpsimd.tensor_tensor(rstd[:, tiles], veps[:, tiles], minus_half[:, tiles], ALU.pow
                                        ).then_inc(rstd_done, 1)
            for c in range(ROUTED):
                for n, u, is_key, pair in qk_units(c):
                    pool.wait_ge(qk_sum, n + 1)
                    nc.gpsimd.tensor_tensor(part_lo[:, u % 4, :], v_sum[:, u % 2, :],
                                            part_hi[:, u % 4, :].bitcast(F32), ALU.subtract).then_inc(qk_lo, 1)
            pool.wait_ge(index_done, 1)
            pool.wait_ge(zero_stored, (ZR + 1) * 16)

            def scatter(i):
                for q in range(2):
                    wait_apart(pool, scattered[q], i * (K * 16), pool_waits)
                    nc.gpsimd.tensor_copy(stage_i[:, q, :], keep["index"][:, bass.ds(2 * i + q, 1), :]
                                          .rearrange("p a k -> p (a k)"))
                    nc.gpsimd.tensor_copy(stage_x[:, q, :], xn[:, bass.ds(2 * i + q, 1), :]
                                          .rearrange("p a d -> p (a d)")).then_inc(staged, 1)
                    wait_apart(pool, staged, 2 * i + q + 1, pool_waits)
                    for k in range(K):
                        nc.gpsimd.indirect_dma_start(
                            out=scr["xbuf"][:, :],
                            out_offset=bass.IndirectOffsetOnAxis(ap=stage_i[:, q, k:k + 1], axis=0),
                            in_=stage_x[:, q, :], in_offset=None,
                            bounds_check=SLOTS - 1, oob_is_err=False).then_inc(scattered[q], 16)
            scatter(0)
            with pool.Fori(1, NT // 2) as i:
                scatter(i)
            for q in range(2):
                pool.wait_ge(scattered[q], NT // 2 * K * 16)

        @block.scalar
        def _(act):
            for n in range(2 * NC):
                act.wait_ge(xt_ready, n + 1)
                nc.scalar.copy(xnT[:, n % 2, (n // 2) * CH:(n // 2 + 1) * CH], ps[:, n % 4, :]
                               ).then_inc(xnT_done, 1)
            for half in range(2):
                act.wait_ge(logits_done, half + 1)
                nc.scalar.activation(score[:, half * 16:half * 16 + 16, :],
                                     ps[:, 4 + half, :].rearrange("p (t e) -> p t e", e=E), ACT.Sigmoid
                                     ).then_inc(score_done, 1)

            def qk_high(c):
                for n, u, is_key, pair in qk_units(c):
                    bias = (bk if is_key else bq)[:, pair:pair + 1]
                    act.wait_ge(qk_ready, n + 1)
                    wait_pos(act, qk_stored[u % 4], (c * 4 + u // 4) * 32)
                    nc.scalar.activation(part_hi[:, u % 4, :], ps[:, 4 + u % 4, :], ACT.Identity, bias=bias
                                         ).then_inc(qk_hi, 1)
                    if isinstance(c, int):
                        wait_pos(act, qk_lo, n - 1)
                        nc.scalar.activation(v_sum[:, u % 2, :], ps[:, 4 + u % 4, :], ACT.Identity, bias=bias
                                             ).then_inc(qk_sum, 1)

            for c in range(ROUTED):
                qk_high(c)
            with act.Fori(ROUTED, NC) as c:
                qk_high(c)
            for n in range(2 * NT):
                act.wait_ge(v_summed, n + 1)
                wait_pos(act, v_stored[n % 2], (n // 2) * 16)
                nc.scalar.copy(v_parts[:, n % 2, :, 0, :],
                               v_sum[:, n % 2, :].rearrange("p (h c) -> p h c", c=DH)).then_inc(v_hi, 1)
            with act.Fori(0, NC) as c:
                for u in range(4):
                    act.wait_ge(gu_ready, c * 4 + u + 1)
                    nc.scalar.activation(silu_g[:, u % 2, :], ps[:, 2 * (u % 2), :], ACT.Silu
                                         ).then_inc(silu_done, 1)

        @block.vector
        def _(dve):
            nc.vector.memset(zeros[:, :], 0.0).then_inc(zero_made, 1)
            for g in range(4):
                tiles = range(g * XG, (g + 1) * XG)
                dve.wait_ge(x_loaded[g], 16)
                for t in tiles:
                    last = nc.vector.bn_stats(stats[:, t, :], x_sb[:, t, :])
                last.then_inc(stats_done, 1)
                dve.wait_ge(stats_done, g + 1)
                for t in tiles:
                    last = nc.vector.bn_aggr(moments[:, t, :], stats[:, t, :])
                last.then_inc(moments_done, 1)
                dve.wait_ge(moments_done, g + 1)
                dve.wait_ge(rstd_done, g + 1)
                for t in tiles:
                    last = nc.vector.tensor_scalar(xn[:, t, :], x_sb[:, t, :], moments[:, t, 0:1],
                                                   rstd[:, t:t + 1], ALU.subtract, ALU.mult)
                    if t % TPC == TPC - 1:
                        last.then_inc(xn_done, 1)

            steps = [0]

            def link(ins):
                steps[0] += 1
                ins.then_inc(route_step, 1)
                dve.wait_ge(route_step, steps[0])

            dve.wait_ge(score_done, 2)
            dve.wait_ge(weights_loaded, N_WEIGHTS * 16)
            link(nc.vector.tensor_tensor(key[:, :, :], score[:, :, :],
                                         eb[:, :].unsqueeze(1).to_broadcast([P, NT, E]), ALU.add))
            for t in range(NT):
                last = nc.vector.max(top[:, t, :], key[:, t, :])
            link(last)
            for t in range(NT):
                last = nc.vector.match_replace(ta[:, t, :], top[:, t, :], key[:, t, :], -3.0e38)
            link(last)
            nc.vector.tensor_tensor(maskb[:, :].rearrange("p (t e) -> p t e", e=E), ta[:, :, :], key[:, :, :],
                                    ALU.not_equal).then_inc(mask_done, 1)
            link(nc.vector.tensor_tensor(mask[:, :, :], ta[:, :, :], key[:, :, :], ALU.not_equal))
            link(nc.vector.tensor_tensor(weight[:, :, :], score[:, :, :], mask[:, :, :], ALU.mult))
            link(nc.vector.tensor_reduce(wsum[:, :], weight[:, :, :], AX.X, ALU.add))
            link(nc.vector.tensor_scalar(wsum[:, :], wsum[:, :], 1e-20, None, ALU.add))
            link(nc.vector.reciprocal(wsum[:, :], wsum[:, :]))
            link(nc.vector.tensor_tensor(weight[:, :, :], weight[:, :, :],
                                         wsum[:, :].unsqueeze(2).to_broadcast([P, NT, E]), ALU.mult))
            nc.vector.tensor_scalar(weight[:, :, :], weight[:, :, :], SCALE, None, ALU.mult)
            dve.wait_ge(counts_done, 1)
            counts = ps[:, 2:4, :].rearrange("p b (t e) -> p (b t) e", e=E)
            within = ps[:, 0:2, :].rearrange("p b (t e) -> p (b t) e", e=E)
            link(nc.vector.tensor_copy(ta[:, :, :], counts))
            a, b = ta, tb
            for s in (1, 2, 4, 8, 16):
                nc.vector.tensor_copy(b[:, 0:s, :], a[:, 0:s, :])
                link(nc.vector.tensor_tensor(b[:, s:NT, :], a[:, s:NT, :], a[:, 0:NT - s, :], ALU.add))
                a, b = b, a
            link(nc.vector.tensor_tensor(b[:, :, :], counts, a[:, :, :], ALU.subtract))
            nc.vector.tensor_tensor(a[:, :, :], within, b[:, :, :], ALU.subtract).then_inc(counts_read, 1)
            dve.wait_ge(counts_read, 1)
            link(nc.vector.scalar_tensor_tensor(out=b[:, :, :], in0=a[:, :, :], scalar=float(CAP),
                                                in1=mask[:, :, :], op0=ALU.is_lt, op1=ALU.mult))
            dve.wait_ge(consts_made, 1)
            link(nc.vector.tensor_tensor(a[:, :, :], a[:, :, :], ebase[:, :, :], ALU.add))
            link(nc.vector.tensor_tensor(key[:, :, :], a[:, :, :], b[:, :, :], ALU.mult))
            for t in range(NT):
                last = nc.vector.max(top[:, t, :], key[:, t, :])
            link(last)
            rows = ta[:, 0:K, :].rearrange("p k e -> p (k e)")
            flat = top[:, :, :].rearrange("p t k -> p (t k)")
            link(nc.vector.tensor_scalar(rows, flat, 0.0, float(SLOTS + 1), ALU.is_equal, ALU.mult))
            nc.vector.scalar_tensor_tensor(out=keep["index"][:, :, :].rearrange("p t k -> p (t k)"), in0=rows,
                                           scalar=-1.0, in1=flat, op0=ALU.add, op1=ALU.add
                                           ).then_inc(index_done, 1)
            dve.wait_ge(index_done, 1)
            for k in range(K):
                link(nc.vector.tensor_tensor(ta[:, :, :], key[:, :, :],
                                             top[:, :, k:k + 1].to_broadcast([P, NT, E]), ALU.is_equal))
                link(nc.vector.tensor_tensor(tb[:, :, :], ta[:, :, :], weight[:, :, :], ALU.mult))
                nc.vector.tensor_reduce(keep["gain"][:, :, k:k + 1], tb[:, :, :], AX.X, ALU.add)
            link(nc.vector.tensor_tensor(x_sb[:, :, :], x_sb[:, :, :],
                                         bo[:, :].unsqueeze(1).to_broadcast([P, NT, D]), ALU.add))

            dve.wait_ge(qk_lo, ROUTED * H)
            with dve.Fori(ROUTED, NC) as c:
                for n, u, is_key, pair in qk_units(c):
                    bias = (bk if is_key else bq)[:, pair:pair + 1]
                    dve.wait_ge(qk_hi, n + 1)
                    nc.vector.scalar_tensor_tensor(out=part_lo[:, u % 4, :], in0=ps[:, 4 + u % 4, :], scalar=bias,
                                                   in1=part_hi[:, u % 4, :].bitcast(F32), op0=ALU.add,
                                                   op1=ALU.subtract).then_inc(qk_lo, 1)

            def v_low(n):
                dve.wait_ge(v_hi, n + 1)
                nc.vector.tensor_tensor(v_parts[:, n % 2, :, 1, :],
                                        v_sum[:, n % 2, :].rearrange("p (h c) -> p h c", c=DH),
                                        v_parts[:, n % 2, :, 0, :].bitcast(F32), ALU.subtract).then_inc(v_lo, 1)

            for n in range(2 * NT):
                dve.wait_ge(v_ready, n + 1)
                wait_pos(dve, v_lo, n - 1)
                nc.vector.tensor_tensor(v_sum[:, n % 2, :], ps[:, n % 4, :],
                                        bv[:, (n % 2) * 512:(n % 2 + 1) * 512], ALU.add).then_inc(v_summed, 1)
                if n:
                    v_low(n - 1)
            v_low(2 * NT - 1)

            def shared(c):
                for u in range(4):
                    dve.wait_ge(silu_done, c * 4 + u + 1)
                    if u == 0:
                        wait_pos(dve, down_ready, c)
                    nc.vector.tensor_tensor(hid[:, u, :], silu_g[:, u % 2, :], ps[:, 2 * (u % 2) + 1, :],
                                            ALU.mult).then_inc(hid_done, 1)
                dve.wait_ge(down_ready, c + 1)
                wait_pos(dve, base_stored, c * 16)
                for h in range(2):
                    last = nc.vector.tensor_tensor(base[:, 2 * h:2 * h + 2, :],
                                                   ps[:, 4 + h, :].rearrange("p (t d) -> p t d", d=D),
                                                   x_sb[:, bass.ds(c * TPC + 2 * h, 2), :], ALU.add)
                last.then_inc(base_done, 1)

            shared(0)
            with dve.Fori(1, NC) as c:
                shared(c)

        @block.tensor
        def _(pe):
            def logits(c):
                pe.wait_ge(xnT_done, 2 * c + 2)
                for t in range(c * TPC, (c + 1) * TPC):
                    out = ps[:, 4 + t // 16, (t % 16) * E:(t % 16 + 1) * E]
                    for k in range(DK):
                        last = nc.tensor.matmul(out, xnT[:, k, t * P:(t + 1) * P], wr[:, k, :],
                                                start=(k == 0), stop=(k == DK - 1))
                    if t % 16 == 15:
                        last.then_inc(logits_done, 1)

            pe.wait_ge(consts_made, 1)
            for c in range(NC):
                pe.wait_ge(xn_done, c + 1)
                for k in range(DK):
                    n = 2 * c + k
                    wait_pos(pe, xnT_done, n - 3)
                    for j in range(TPC):
                        last = nc.tensor.transpose(ps[:, n % 4, j * P:(j + 1) * P],
                                                   xn[:, c * TPC + j, k * P:(k + 1) * P], keep["ident"][:, :])
                    last.then_inc(xt_ready, 1)
                if c == 0:
                    pe.wait_ge(wr_loaded, 16)
                if c:
                    logits(c - 1)
            logits(NC - 1)

            def counts():
                pe.wait_ge(mask_done, 1)
                for h in range(2):
                    nc.tensor.matmul(ps[:, h, :], earlier[:, :], maskb[:, h * 512:(h + 1) * 512],
                                     start=True, stop=True)
                    last = nc.tensor.matmul(ps[:, 2 + h, :], onesb[:, :], maskb[:, h * 512:(h + 1) * 512],
                                            start=True, stop=True)
                last.then_inc(counts_done, 1)

            pe.wait_ge(weights_loaded, N_WEIGHTS * 16)
            pe.wait_ge(score_done, 2)
            def qk(c):
                for n, u, is_key, pair in qk_units(c):
                    w = wk if is_key else wq
                    wait_pos(pe, qk_lo, n - 3)
                    for k in range(DK):
                        last = nc.tensor.matmul(ps[:, 4 + u % 4, :], w[:, k, pair * P:(pair + 1) * P],
                                                xnT[:, k, bass.ds(c * CH, CH)],
                                                start=(k == 0), stop=(k == DK - 1))
                    last.then_inc(qk_ready, 1)
                    if isinstance(c, int) and u == COUNTS_AT:
                        counts()

            qk(0)
            with pe.Fori(1, NC) as c:
                qk(c)
            pe.wait_ge(counts_read, 1)
            for n in range(2 * NT):
                t, half = n // 2, n % 2
                wait_pos(pe, v_summed, n - 3)
                for k in range(DK):
                    last = nc.tensor.matmul(ps[:, n % 4, :], xnT[:, k, t * P:(t + 1) * P],
                                            wv[:, k, half * 512:(half + 1) * 512],
                                            start=(k == 0), stop=(k == DK - 1))
                last.then_inc(v_ready, 1)

            def gate_up(c, u):
                wait_pos(pe, hid_done, c * 4 + u - 1)
                for bank, w in ((2 * (u % 2), wg), (2 * (u % 2) + 1, wu)):
                    for k in range(DK):
                        last = nc.tensor.matmul(ps[:, bank, :], w[:, k, u * P:(u + 1) * P],
                                                xnT[:, k, bass.ds(c * CH, CH)],
                                                start=(k == 0), stop=(k == DK - 1))
                last.then_inc(gu_ready, 1)

            def shared(c, following):
                for u in range(1, 4):
                    gate_up(c, u)
                if following:
                    gate_up(c + 1, 0)
                pe.wait_ge(hid_done, c * 4 + 4)
                wait_pos(pe, base_done, c)
                for j in range(TPC):
                    for u in range(4):
                        last = nc.tensor.matmul(ps[:, 4 + j // 2, (j % 2) * D:(j % 2 + 1) * D],
                                                hid[:, u, j * P:(j + 1) * P], wd[:, u, :],
                                                start=(u == 0), stop=(u == 3))
                last.then_inc(down_ready, 1)

            pe.wait_ge(v_summed, 2 * NT)
            pe.wait_ge(qk_lo, NC * H)
            gate_up(0, 0)
            shared(0, True)
            with pe.Fori(1, NC - 1) as c:
                shared(c, True)
            shared(NC - 1, False)




def run_experts(nc, io, scr, keep):
    with ExitStack() as stack:
        m = Memory(nc, stack, "ex")
        ps = m.ps("ps", [P, 8, CH])
        CT = CAP // P
        xe = m.sb("xe", [P, 2, CT, D])
        xeT = m.sb("xeT", [P, 2, DK, CAP])
        gu = m.sb("gu", [P, 2, DK, 2 * I])
        dn = m.sb("dn", [P, 2, D])
        gate = m.sb("gate", [P, 2, CAP])
        up = m.sb("up", [P, 2, CAP])
        silu_g = m.sb("silu_g", [P, 2, CAP])
        hid = m.sb("hid", [P, 2, CAP])
        dn_old = m.sb("dn_old", [P, 2, D])
        ye = m.sb("ye", [P, 2, CT, D])

        loaded = m.sems("loaded", 2)
        turned = m.sem("turned")
        xeT_done = m.sem("xeT_done")
        gu_ready = m.sem("gu_ready")
        gate_done = m.sem("gate_done")
        up_done = m.sem("up_done")
        silu_done = m.sem("silu_done")
        hid_done = m.sem("hid_done")
        dn_kept = m.sem("dn_kept")
        down_ready = m.sem("down_ready")
        ye_done = m.sem("ye_done")
        stored = m.sems("stored", 2)
        sp_waits, pool_waits = m.sem("sp_waits"), m.sem("pool_waits")
        block = stack.enter_context(nc.Block())

        @block.sync
        def _(sp):
            def load(i):
                for q in range(2):
                    e = 2 * i + q
                    wait_apart(sp, turned, 2 * i + q - 1, sp_waits)
                    wait_apart(sp, gu_ready, 2 * i + q - 1, sp_waits)
                    wait_apart(sp, dn_kept, 2 * i + q - 1, sp_waits)
                    sp.dma_start(xe[:, q, :, :], scr["xbuf"][bass.ds(e * CAP, CAP), :]
                                 .rearrange("(t p) d -> p t d", p=P)).then_inc(loaded[q], 16)
                    sp.dma_start(gu[:, q, :, :], io["gu"][bass.ds(e, 1), :, :, :]
                                 .rearrange("a p k o -> p (a k) o")).then_inc(loaded[q], 16)
                    sp.dma_start(dn[:, q, :], io["dn"][bass.ds(e, 1), :, :]
                                 .rearrange("a p d -> p (a d)")).then_inc(loaded[q], 16)

            load(0)
            with sp.Fori(1, E // 2) as i:
                load(i)

        @block.gpsimd
        def _(pool):
            def store(i):
                for q in range(2):
                    e = 2 * i + q
                    wait_apart(pool, ye_done, 2 * i + q + 1, pool_waits)
                    pool.dma_start(scr["ye"][bass.ds(e * CAP, CAP), :].rearrange("(t p) d -> p t d", p=P),
                                   ye[:, q, :, :]).then_inc(stored[q], 16)

            with pool.Fori(0, E // 2) as i:
                store(i)
            for q in range(2):
                pool.wait_ge(stored[q], E // 2 * 16)

        @block.scalar
        def _(act):
            def turn(i, q):
                n = 2 * i + q
                act.wait_ge(turned, n + 1)
                nc.scalar.copy(xeT[:, q, :, :], ps[:, 0:2, :]).then_inc(xeT_done, 1)

            def down(i, q):
                n = 2 * i + q
                act.wait_ge(down_ready, n + 1)
                wait_pos(act, stored[q], i * 16)
                nc.scalar.copy(ye[:, q, :, :].rearrange("p t d -> p (t d)"),
                               ps[:, 2:4, :].rearrange("p b c -> p (b c)")).then_inc(ye_done, 1)

            def silu(i, q):
                n = 2 * i + q
                act.wait_ge(gate_done, n + 1)
                nc.scalar.activation(silu_g[:, q, :], gate[:, q, :], ACT.Silu).then_inc(silu_done, 1)

            for q in range(2):
                turn(0, q)
                silu(0, q)

            def both(i):
                for q in range(2):
                    turn(i, q)
                    down(i - 1, q)
                    silu(i, q)

            both(1)
            with act.Fori(2, E // 2) as i:
                both(i)
            for q in range(2):
                down(E // 2 - 1, q)

        @block.vector
        def _(dve):
            def hidden(i):
                for q in range(2):
                    n = 2 * i + q
                    dve.wait_ge(gu_ready, n + 1)
                    wait_pos(dve, down_ready, n - 1)
                    nc.vector.tensor_copy(dn_old[:, q, :], dn[:, q, :]).then_inc(dn_kept, 1)
                    nc.vector.tensor_scalar(gate[:, q, :], ps[:, 4 + 2 * q, :], LIMIT, None, ALU.min
                                            ).then_inc(gate_done, 1)
                    nc.vector.tensor_scalar(up[:, q, :], ps[:, 5 + 2 * q, :], LIMIT, -LIMIT, ALU.min, ALU.max
                                            ).then_inc(up_done, 1)
                    dve.wait_ge(up_done, n + 1)
                    dve.wait_ge(silu_done, n + 1)
                    nc.vector.tensor_tensor(hid[:, q, :], silu_g[:, q, :], up[:, q, :], ALU.mult
                                            ).then_inc(hid_done, 1)

            hidden(0)
            with dve.Fori(1, E // 2) as i:
                hidden(i)

        @block.tensor
        def _(pe):
            def turn(i, q):
                pe.wait_ge(loaded[q], i * 48 + 48)
                wait_pos(pe, xeT_done, 2 * i + q)
                for k in range(DK):
                    for t in range(CT):
                        last = nc.tensor.transpose(ps[:, k, t * P:(t + 1) * P],
                                                   xe[:, q, t, k * P:(k + 1) * P], keep["ident"][:, :])
                last.then_inc(turned, 1)

            def gate_up(i, q):
                n = 2 * i + q
                pe.wait_ge(xeT_done, n + 1)
                wait_pos(pe, up_done, n - 1)
                for side in range(2):
                    for k in range(DK):
                        last = nc.tensor.matmul(ps[:, 4 + 2 * q + side, :], gu[:, q, k, side * I:(side + 1) * I],
                                                xeT[:, q, k, :], start=(k == 0), stop=(k == DK - 1))
                last.then_inc(gu_ready, 1)

            def down(i, q):
                n = 2 * i + q
                pe.wait_ge(hid_done, n + 1)
                pe.wait_ge(dn_kept, n + 1)
                wait_pos(pe, ye_done, n)
                for t in range(CT):
                    last = nc.tensor.matmul(ps[:, 2 + t // 2, (t % 2) * D:(t % 2 + 1) * D],
                                            hid[:, q, t * P:(t + 1) * P], dn_old[:, q, :], start=True, stop=True)
                last.then_inc(down_ready, 1)

            for q in range(2):
                turn(0, q)
                gate_up(0, q)
            def both(i):
                for q in range(2):
                    turn(i, q)
                    down(i - 1, q)
                    gate_up(i, q)

            both(1)
            with pe.Fori(2, E // 2) as i:
                both(i)
            for q in range(2):
                down(E // 2 - 1, q)



GT = 4
TILES = T // P
GROUPS = TILES // GT
PV_LAG = GT + 1
OUT_LAG = 2 * GT + 1
LAST = OUT_LAG + TILES
BANK = (4, 5, 7, 7)
FREED = (4, 4, 3, 1)
OUT_BANK = 4
BACK = (1, 1, 1, 2)


def attend(nc, io, scr, keep):
    with ExitStack() as stack:
        m = Memory(nc, stack, "at")
        ps = m.ps("ps", [P, 8, CH])
        q_hh = m.sb("q_hh", [P, 2, CH], F32R)
        q_ll = m.sb("q_ll", [P, 2, CH], F32R)
        k_hl = m.sb("k_hl", [P, 2, T], F32R)
        v_hl = m.sb("v_hl", [P, NS, P], F32R)
        wo = m.sb("wo", [P, 2, D])
        prob = m.sb("prob", [P, 2, T])
        pT_hi = m.sb("pT_hi", [P, 2, NS, CH], F32R)
        pT_lo = m.sb("pT_lo", [P, 2, NS, CH], F32R)
        oT = m.sb("oT", [P, 2, CH])
        acc = m.sb("acc", [P, TILES, D])
        half_max = m.sb("half_max", [P, 2, 2])
        neg_max = m.sb("neg_max", [P, 2])
        half_sum = m.sb("half_sum", [P, TILES, 2])
        total = m.sb("total", [P, TILES])
        inv = m.sb("inv", [P, TILES])

        g_index = m.sb("g_index", [P, K], U32)
        g_gain = m.sb("g_gain", [P, K])
        rows = m.sb("rows", [P, 4, D])
        rest = m.sb("rest", [P, D])
        rest_t = rows[:, 0:2, :]

        q_loaded = m.sems("q_loaded", 2)
        k_loaded = m.sems("k_loaded", 2)
        v_loaded = m.sems("v_loaded", GT)
        wo_loaded = m.sems("wo_loaded", 2)
        scored = m.sem("scored")
        max_step = m.sem("max_step")
        max_done = m.sem("max_done")
        exp_done = m.sem("exp_done")
        turned = m.sem("turned")
        high_done = m.sem("high_done")
        low_done = m.sem("low_done")
        pv_done = m.sem("pv_done")
        oT_done = m.sem("oT_done")
        sum_step = m.sem("sum_step")
        inv_done = m.sem("inv_done")
        projected = m.sem("projected")
        cleared = m.sem("cleared")
        added = m.sem("added")
        rest_loaded = m.sems("rest_loaded", 2)
        finished = m.sem("finished")
        stored = m.sem("stored")
        restarted = m.sem("restarted")
        out_stored = m.sem("out_stored")
        g_staged = m.sem("g_staged")
        g_base = m.sem("g_base")
        gathered = m.sem("gathered")
        g_step = m.sem("g_step")
        g_stored = m.sem("g_stored")
        sp_waits, pool_waits = m.sem("sp_waits"), m.sem("pool_waits")
        block = stack.enter_context(nc.Block())

        def slots(b, h):
            head = b * H + h
            opens = b == 0 and isinstance(h, int) and h == 0
            for s in range(LAST if b == B - 1 and isinstance(h, int) and h == H - 1 else TILES):
                tile = head * TILES + s
                back = [(s - 1) // GT, (s - PV_LAG) // GT, (s - OUT_LAG) // GT]
                turn = not opens or s >= 1
                late = not opens or s >= 2
                pv = not opens or s >= PV_LAG
                out = not opens or s >= OUT_LAG
                yield dict(
                    s=s, head=head, tile=tile, scores=s < TILES, turn=turn and s <= TILES,
                    late=late and s <= TILES + 1,
                    pv=(head * GROUPS + back[1], back[1] % 2, (s - PV_LAG) % GT)
                    if pv and s < PV_LAG + TILES else None,
                    out=(head * GROUPS + back[2], back[2] % GROUPS, (s - OUT_LAG) % GT, s < OUT_LAG)
                    if out and s < OUT_LAG + TILES else None)

        def over_heads(eng, body):
            for b in range(B):
                for s in slots(b, 0):
                    body(b, 0, s)
                with eng.Fori(1, H - 1) as h:
                    for s in slots(b, h):
                        body(b, h, s)
                for s in slots(b, H - 1):
                    body(b, H - 1, s)

        @block.sync
        def _(sp):
            def load_q(b, h, g):
                group = (b * H + h) * GROUPS + g
                wait_apart(sp, scored, 2 * GT * (group - 1), sp_waits)
                for part, dst in ((0, q_hh), (1, q_ll)):
                    src = scr["q"][part, bass.ds(h * DH, DH), b * T + g * CH:b * T + (g + 1) * CH]
                    for rows_ in (slice(0, DH), slice(DH, P)):
                        sp.dma_start(dst[rows_, g % 2, :].bitcast(F32), src).then_inc(q_loaded[g % 2], 16)

            def load_k(b, h, side):
                head = b * H + h
                wait_apart(sp, scored, 2 * ((head - 1) * TILES + (side + 1) * TILES // 2), sp_waits)
                for part in range(2):
                    sp.dma_start(k_hl[part * DH:(part + 1) * DH, side, :].bitcast(F32),
                                 scr["k"][part, bass.ds(h * DH, DH), b * T:(b + 1) * T]).then_inc(k_loaded[side], 16)

            def load_v(b, h, quarter):
                wait_apart(sp, pv_done, GT * ((b * H + h) * GROUPS - 1) + quarter + 1, sp_waits)
                tiles = slice(quarter * GT, (quarter + 1) * GT)
                sp.dma_start(v_hl[:, tiles, :].bitcast(F32),
                             scr["v"][bass.ds(h, 1), :, b * NS + quarter * GT:b * NS + (quarter + 1) * GT, :]
                             .rearrange("a p t c -> p (a t) c")).then_inc(v_loaded[quarter], 16)

            def load_wo(b, h, side):
                wait_apart(sp, projected, (b * H + h) * TILES - TILES // 2 * (1 - side), sp_waits)
                sp.dma_start(wo[:, side, :], io["wo"][bass.ds(h, 1), :, :].rearrange("a p d -> p (a d)")
                             ).then_inc(wo_loaded[side], 16)

            def head_loads(b, h, following):
                load_q(b, h, 1)
                load_k(b, h, 1)
                load_wo(b, h, 0)
                for quarter in range(GT):
                    load_v(b, h, quarter)
                load_q(b, h, 2)
                load_q(b, h, 3)
                load_wo(b, h, 1)
                if following is not None:
                    load_k(*following, 0)
                    load_q(*following, 0)

            load_k(0, 0, 0)
            load_q(0, 0, 0)
            for b in range(B):
                head_loads(b, 0, (b, 1))
                with sp.Fori(1, H - 1) as h:
                    head_loads(b, h, (b, h + 1))
                head_loads(b, H - 1, (b + 1, 0) if b + 1 < B else None)
            for t in range(TILES):
                sp.wait_ge(added, (B * H - 1) * TILES + t + 1)
                sp.dma_start(io["out"][(NT - TILES + t) * P:(NT - TILES + t + 1) * P, :], acc[:, t, :]
                             ).then_inc(out_stored, 16)
            sp.wait_ge(out_stored, TILES * 16)

        @block.gpsimd
        def _(pool):
            def gather(n, k):
                nc.gpsimd.indirect_dma_start(
                    out=rows[:, k % 4, :], out_offset=None, in_=scr["ye"][:, :],
                    in_offset=bass.IndirectOffsetOnAxis(ap=g_index[:, k:k + 1], axis=0),
                    bounds_check=SLOTS, oob_is_err=True).then_inc(gathered, 16)

            with pool.Fori(0, NT) as n:
                nc.gpsimd.tensor_copy(g_index[:, :], keep["index"][:, bass.ds(n, 1), :]
                                      .rearrange("p a k -> p (a k)"))
                nc.gpsimd.tensor_copy(g_gain[:, :], keep["gain"][:, bass.ds(n, 1), :]
                                      .rearrange("p a k -> p (a k)")).then_inc(g_staged, 1)
                pool.dma_start(rest[:, :], scr["base"][:, bass.ds(n, 1), :].rearrange("p a d -> p (a d)")
                               ).then_inc(g_base, 16)
                wait_apart(pool, g_staged, n + 1, pool_waits)
                for r in range(2):
                    for k in range(4 * r, 4 * r + 4):
                        gather(n, k)
                    if r == 0:
                        wait_apart(pool, g_base, n * 16 + 16, pool_waits)
                    wait_apart(pool, gathered, n * (K * 16) + (r + 1) * 64, pool_waits)
                    for k in range(4):
                        nc.gpsimd.tensor_scalar(rows[:, k, :], rows[:, k, :], g_gain[:, 4 * r + k:4 * r + k + 1],
                                                None, ALU.mult).then_inc(g_step, 1)
                        wait_apart(pool, g_step, n * (2 * K) + 8 * r + 2 * k + 1, pool_waits)
                        nc.gpsimd.tensor_tensor(rest[:, :], rest[:, :], rows[:, k, :], ALU.add).then_inc(g_step, 1)
                        wait_apart(pool, g_step, n * (2 * K) + 8 * r + 2 * k + 2, pool_waits)
                pool.dma_start(scr["rest"][:, bass.ds(n, 1), :].rearrange("p a d -> p (a d)"), rest[:, :]
                               ).then_inc(g_stored, 16)
                wait_apart(pool, g_stored, n * 16 + 16, pool_waits)
            for t in range(2):
                pool.dma_start(rest_t[:, t, :], scr["rest"][:, t, :]).then_inc(rest_loaded[t], 16)
            for t in range(TILES):
                pool.wait_ge(finished, t + 1)
                pool.dma_start(io["out"][t * P:(t + 1) * P, :], acc[:, t, :]).then_inc(stored, 16)
                if t + 2 < TILES:
                    pool.dma_start(rest_t[:, t % 2, :], scr["rest"][:, t + 2, :]).then_inc(rest_loaded[t % 2], 16)
                pool.wait_ge(stored, 16 * (t + 1))
                pool.dma_start(acc[:, t, :], scr["rest"][:, TILES + t, :]).then_inc(restarted, 16)

        @block.tensor
        def _(pe):
            def transpose(s, unit):
                n = (s["tile"] - BACK[unit]) * GT + unit
                if unit % 2 == 0:
                    pe.wait_ge(exp_done, 2 * s["tile"] - 1 + unit // 2)
                wait_pos(pe, low_done, n + 1 - FREED[unit])
                if BANK[unit] == OUT_BANK and s["out"]:
                    wait_pos(pe, added, s["out"][0] * GT + s["out"][2])
                for j in range(GT):
                    t = unit * GT + j
                    last = nc.tensor.transpose(ps[:, BANK[unit], j * P:(j + 1) * P],
                                               prob[:, (s["s"] - BACK[unit]) % 2, t * P:(t + 1) * P], keep["ident"][:, :])
                last.then_inc(turned, 1)

            def score(s, half):
                i, head = s["s"], s["head"]
                g, j, side = i // GT, i % GT, i // (TILES // 2)
                if half == 0 and j == 0:
                    pe.wait_ge(q_loaded[g % 2], 64 * (head * 2 + g // 2) + 64)
                if half == 0 and i % (TILES // 2) == 0:
                    pe.wait_ge(k_loaded[side], 32 * head + 32)
                wait_pos(pe, exp_done, 2 * s["tile"] - 1 + half)
                for c in (2 * half, 2 * half + 1):
                    for q, first in ((q_hh, True), (q_ll, False)):
                        last = nc.tensor.matmul(ps[:, c, :], q[:, g % 2, j * P:(j + 1) * P],
                                                k_hl[:, side, c * CH:(c + 1) * CH],
                                                start=first, stop=not first)
                last.then_inc(scored, 1)

            def times_v(s, first, last_):
                group, parity, quarter = s["pv"]
                if first == 0:
                    pe.wait_ge(low_done, group * (GT * GT) + (GT - 1) * GT + quarter + 1)
                    pe.wait_ge(v_loaded[quarter],
                               16 * (s["head"] + (1 if s["s"] >= PV_LAG and s["s"] < TILES + PV_LAG else 0)))
                    if quarter == 0:
                        wait_pos(pe, oT_done, group)
                for t in range(quarter * GT + first, quarter * GT + last_):
                    for part in (pT_hi, pT_lo):
                        last = nc.tensor.matmul(ps[:, 6, :], v_hl[:, t, :], part[:, parity, t, :],
                                                start=(t == 0 and part is pT_hi),
                                                stop=(t == NS - 1 and part is pT_lo))
                if last_ == GT:
                    last.then_inc(pv_done, 1)

            def project(s):
                group, g, j, behind = s["out"]
                n = group * GT + j
                if j == 0:
                    pe.wait_ge(oT_done, group + 1)
                    pe.wait_ge(wo_loaded[g // 2], 16 * (s["head"] + (0 if behind else 1)))
                wait_pos(pe, added, n)
                if s["turn"]:
                    pe.wait_ge(low_done, (s["tile"] - 1) * GT + 1)
                nc.tensor.matmul(ps[:, OUT_BANK, 0:D], oT[:, g % 2, j * P:(j + 1) * P], wo[:, g // 2, :],
                                 start=True, stop=True).then_inc(projected, 1)

            def body(b, h, s):
                if s["scores"]:
                    score(s, 0)
                if s["late"]:
                    transpose(s, 3)
                if s["turn"]:
                    transpose(s, 0)
                if s["scores"]:
                    score(s, 1)
                if s["turn"]:
                    transpose(s, 1)
                    transpose(s, 2)
                if s["pv"]:
                    times_v(s, 0, GT)
                if s["out"]:
                    project(s)

            over_heads(pe, body)

        @block.scalar
        def _(act):
            def high(s, unit):
                i = s["s"] - BACK[unit]
                n = (s["tile"] - BACK[unit]) * GT + unit
                act.wait_ge(turned, n + 1)
                nc.scalar.copy(pT_hi[:, i // GT % 2, unit * GT:(unit + 1) * GT, i % GT * P:(i % GT + 1) * P],
                               ps[:, BANK[unit], :].rearrange("p (t c) -> p t c", c=P)).then_inc(high_done, 1)

            def exponent(s, half):
                i, tile = s["s"], s["tile"]
                if half == 0:
                    act.wait_ge(max_done, tile + 1)
                wait_pos(act, turned, GT * (tile - 2) + 2 * half + 2)
                nc.scalar.activation(prob[:, i % 2, half * 1024:(half + 1) * 1024],
                                     ps[:, 2 * half:2 * half + 2, :].rearrange("p b c -> p (b c)"),
                                     ACT.Exp, bias=neg_max[:, i % 2:i % 2 + 1], scale=DH ** -0.5,
                                     accum_out=half_sum[:, i % TILES, half:half + 1]).then_inc(exp_done, 1)

            def body(b, h, s):
                if s["late"]:
                    high(s, 3)
                if s["turn"]:
                    for unit in range(3):
                        high(s, unit)
                if s["scores"]:
                    exponent(s, 0)
                    exponent(s, 1)
                if s["pv"] and s["pv"][2] == GT - 1:
                    group, parity, _ = s["pv"]
                    act.wait_ge(pv_done, GT * (group + 1))
                    wait_pos(act, projected, GT * (group - 1))
                    nc.scalar.copy(oT[:, parity, :], ps[:, 6, :]).then_inc(oT_done, 1)

            over_heads(act, body)

        @block.vector
        def _(dve):
            def low(s, unit):
                i = s["s"] - BACK[unit]
                n = (s["tile"] - BACK[unit]) * GT + unit
                dve.wait_ge(high_done, n + 1)
                where = (slice(None), i // GT % 2, slice(unit * GT, (unit + 1) * GT), slice(i % GT * P, (i % GT + 1) * P))
                nc.vector.tensor_tensor(pT_lo[where], ps[:, BANK[unit], :].rearrange("p (t c) -> p t c", c=P),
                                        pT_hi[where].bitcast(F32), ALU.subtract).then_inc(low_done, 1)

            def maximum(s, half):
                i, tile = s["s"], s["tile"]
                dve.wait_ge(scored, 2 * tile + half + 1)
                nc.vector.tensor_reduce(half_max[:, i % 2, half:half + 1], ps[:, 2 * half:2 * half + 2, :],
                                        AX.XY, ALU.max).then_inc(max_step, 1)
                if half == 1:
                    dve.wait_ge(max_step, 2 * tile + 2)
                    wait_pos(dve, exp_done, 2 * (tile - 1))
                    nc.vector.tensor_scalar(neg_max[:, i % 2:i % 2 + 1], half_max[:, i % 2, 0:1],
                                            half_max[:, i % 2, 1:2], -(DH ** -0.5), ALU.max, ALU.mult
                                            ).then_inc(max_done, 1)

            def body(b, h, s):
                i, tile, head = s["s"], s["tile"], s["head"]
                first = isinstance(h, int) and h == 0
                if first and b == 0 and i == 0:
                    nc.vector.memset(acc[:, :, :], 0.0).then_inc(cleared, 1)
                if s["scores"]:
                    maximum(s, 0)
                if s["late"]:
                    low(s, 3)
                if s["scores"]:
                    maximum(s, 1)
                if s["turn"]:
                    for unit in range(3):
                        low(s, unit)
                if s["out"]:
                    group, g, j, behind = s["out"]
                    n, t = group * GT + j, g * GT + j
                    dve.wait_ge(projected, n + 1)
                    if j == 0:
                        dve.wait_ge(inv_done, group + 1)
                    if first and b == 0 and i == OUT_LAG:
                        dve.wait_ge(cleared, 1)
                    if first and b == 1 and i >= OUT_LAG:
                        dve.wait_ge(restarted, 16 * (t + 1 if i < TILES - 1 else TILES))
                    wait_pos(dve, added, n - TILES // 2 + 1)
                    nc.vector.scalar_tensor_tensor(out=acc[:, t, :], in0=ps[:, OUT_BANK, 0:D], scalar=inv[:, t:t + 1],
                                                   in1=acc[:, t, :], op0=ALU.mult, op1=ALU.add
                                                   ).then_inc(added, 1)
                    if isinstance(head, int) and (head - behind + 1) == H:
                        dve.wait_ge(rest_loaded[t % 2], 16 * (t // 2 + 1))
                        dve.wait_ge(added, n + 1)
                        nc.vector.tensor_tensor(acc[:, t, :], acc[:, t, :], rest_t[:, t % 2, :], ALU.add
                                                ).then_inc(finished, 1)
                if s["pv"] and s["pv"][2] == 0:
                    group = s["pv"][0]
                    g = (s["s"] - PV_LAG) // GT % GROUPS
                    tiles = slice(g * GT, (g + 1) * GT)
                    dve.wait_ge(exp_done, 2 * GT * (group + 1))
                    nc.vector.tensor_tensor(total[:, tiles], half_sum[:, tiles, 0], half_sum[:, tiles, 1], ALU.add
                                            ).then_inc(sum_step, 1)
                    dve.wait_ge(sum_step, group + 1)
                    nc.vector.reciprocal(inv[:, tiles], total[:, tiles]).then_inc(inv_done, 1)

            over_heads(dve, body)


def build(nc, io):
    scr = {
        "xbuf": nc.dram_tensor("xbuf", (SLOTS, D), F32, kind="Internal").ap(),
        "ye": nc.dram_tensor("ye", (SLOTS + P, D), F32, kind="Internal").ap(),
        "q": nc.dram_tensor("q_parts", (2, H * DH, TOK), F32, kind="Internal").ap(),
        "k": nc.dram_tensor("k_parts", (2, H * DH, TOK), F32, kind="Internal").ap(),
        "v": nc.dram_tensor("v_parts", (H, P, NT, P), F32, kind="Internal").ap(),
        "base": nc.dram_tensor("base", (P, NT, D), F32, kind="Internal").ap(),
        "rest": nc.dram_tensor("rest", (P, NT, D), F32, kind="Internal").ap(),
    }
    with ExitStack() as stack:
        m = Memory(nc, stack, "keep")
        keep = {
            "ident": m.sb("ident", [P, P]),
            "index": m.sb("index", [P, NT, K], U32),
            "gain": m.sb("gain", [P, NT, K]),
        }
        project_and_route(nc, io, scr, keep)
        run_experts(nc, io, scr, keep)
        attend(nc, io, scr, keep)


def kernel(**inputs):
    import numpy as np
    import concourse.bacc as bacc
    from concourse.bass_utils import run_bass_kernel_spmd

    a = {n: np.asarray(v) for n, v in inputs.items()}

    def halves(w):
        return w.T.reshape(DK, P, -1).transpose(1, 0, 2)

    wo = a["L0_attn_W_O"].transpose(0, 2, 1)
    gu = a["L0_ffn_gate_up_proj"].transpose(0, 2, 1).reshape(E, DK, P, 2 * I)
    laid = {
        "x": a["L0_attn_x"].reshape(TOK, D),
        "wq": halves(a["L0_attn_W_Q"].reshape(H * DH, D)),
        "wk": halves(a["L0_attn_W_K"].reshape(H * DH, D)),
        "wv": halves(a["L0_attn_W_V"].reshape(H * DH, D)),
        "bq": a["L0_attn_b_Q"].reshape(H // 2, P).T,
        "bk": a["L0_attn_b_K"].reshape(H // 2, P).T,
        "bv": a["L0_attn_b_V"].reshape(H * DH),
        "bo": a["L0_attn_b_O"],
        "wo": np.concatenate([wo, wo], axis=1),
        "wr": halves(a["L0_ffn_router_weight"]),
        "eb": a["L0_ffn_e_score_correction_bias"],
        "gu": gu.transpose(0, 2, 1, 3),
        "dn": a["L0_ffn_down_proj"].transpose(0, 2, 1),
        "wg": halves(a["L0_ffn_shared_gate"]),
        "wu": halves(a["L0_ffn_shared_up"]),
        "wd": a["L0_ffn_shared_down"].T.reshape(SI // P, P, D).transpose(1, 0, 2),
    }
    nc = bacc.Bacc("TRN2", target_bir_lowering=False, num_devices=1)
    arrays, io = {}, {}
    for name, v in laid.items():
        v = np.ascontiguousarray(v)
        arrays[f"in_{name}"] = v
        io[name] = nc.dram_tensor(f"in_{name}", v.shape, mybir.dt.from_np(v.dtype), kind="ExternalInput").ap()
    io["out"] = nc.dram_tensor("out", (TOK, D), F32, kind="ExternalOutput").ap()
    build(nc, io)
    r = run_bass_kernel_spmd(nc, [arrays], core_ids=[0])
    return r.results[0]["out"].reshape(B, T, D)
```

```python
from contextlib import ExitStack

import concourse.bass as bass
from concourse import mybir

F32 = mybir.dt.float32
F32R = mybir.dt.float32r
BF16 = mybir.dt.bfloat16
U32 = mybir.dt.uint32
ALU = mybir.AluOpType
ACT = mybir.ActivationFunctionType
AX = mybir.AxisListType

P = 128
B, T, D = 2, 2048, 256
TOK = B * T
NT = TOK // P
DK = D // P
H, DH = 16, 64
E, K = 32, 8
I, SI = 128, 512
CAP = 512
LIMIT, SCALE, EPS = 7.0, 2.5, 1e-5
CH = 512
NC = TOK // CH
TPC = CH // P
NS = T // P
SLOTS = E * CAP


def wait_pos(eng, sem, value):
    if not isinstance(value, int) or value > 0:
        eng.wait_ge(sem, value)


def wait_apart(eng, sem, value, passed):
    if isinstance(value, int):
        wait_pos(eng, sem, value)
    else:
        eng.wait_ge(sem, value)
        eng.sem_inc(passed, 1)


class Memory:

    def __init__(self, nc, stack, tag):
        self.nc, self.stack, self.tag = nc, stack, tag

    def sb(self, name, shape, dt=F32):
        return self.stack.enter_context(self.nc.sbuf_tensor(f"{self.tag}_{name}", shape, dt))

    def ps(self, name, shape, dt=F32):
        return self.stack.enter_context(self.nc.psum_tensor(f"{self.tag}_{name}", shape, dt))

    def sem(self, name):
        return self.stack.enter_context(self.nc.semaphore(f"{self.tag}_{name}"))

    def sems(self, name, n):
        return [self.sem(f"{name}{i}") for i in range(n)]




def project_and_route(nc, io, scr, keep, ahead):
    with ExitStack() as stack:
        m = Memory(nc, stack, "pr")
        ps = m.ps("ps", [P, 8, CH])

        x_sb = m.sb("x", [P, NT, D])
        xn = m.sb("xn", [P, NT, D])
        xnT = m.sb("xnT", [P, DK, TOK])
        wq = m.sb("wq", [P, DK, H * DH])
        wk = m.sb("wk", [P, DK, H * DH])
        wv = m.sb("wv", [P, DK, H * DH])
        wg = m.sb("wg", [P, DK, SI])
        wu = m.sb("wu", [P, DK, SI])
        wd = m.sb("wd", [P, SI // P, D])
        wr = m.sb("wr", [P, DK, E])
        bq = m.sb("bq", [P, H // 2])
        bk = m.sb("bk", [P, H // 2])
        bv = m.sb("bv", [P, H * DH])
        bo = m.sb("bo", [P, D])
        eb = m.sb("eb", [P, E])

        stats = m.sb("stats", [P, NT, 6])
        moments = m.sb("moments", [P, NT, 2])
        veps = m.sb("veps", [P, NT])
        minus_half = m.sb("minus_half", [P, NT])
        rstd = m.sb("rstd", [P, NT])

        score = m.sb("score", [P, NT, E])
        mask = m.sb("mask", [P, NT, E])
        weight = m.sb("weight", [P, NT, E])
        key = m.sb("key", [P, NT, E])
        ebase = m.sb("ebase", [P, NT, E])
        tables = m.sb("tables", [P, 2, NT, E])
        ta, tb = tables[:, 0, :, :], tables[:, 1, :, :]
        maskb = m.sb("maskb", [P, NT * E], BF16)
        top = m.sb("top", [P, NT, K])
        wsum = m.sb("wsum", [P, NT])
        earlier = m.sb("earlier", [P, P], BF16)
        onesb = m.sb("onesb", [P, P], BF16)

        stage_i = m.sb("stage_i", [P, 2, K], U32)
        part_hi = m.sb("part_hi", [P, 4, CH], F32R)
        part_lo = m.sb("part_lo", [P, 4, CH], F32R)
        v_sum = m.sb("v_sum", [P, 2, 512])
        zeros = v_sum[:, :, :].rearrange("p u c -> p (u c)")
        v_parts = [part[:, 2 * i:2 * i + 2, :].rearrange("p u c -> p (u c)")
                   .rearrange("p (h a c) -> p h a c", a=2, c=DH) for part in (part_hi, part_lo) for i in range(2)]
        silu_g = score[:, :, :].rearrange("p t e -> p (t e)").rearrange("p (u c) -> p u c", c=CH)
        hid = tables[:, :, :, :].rearrange("p a t e -> p (a t e)").rearrange("p (u c) -> p u c", c=CH)
        stage_x = ebase[:, 0:2 * D // E, :].rearrange("p t e -> p (t e)").rearrange("p (q d) -> p q d", d=D)
        qk_sums = ahead["xe"][:, :, 0:CH // D, :].rearrange("p q t d -> p q (t d)")
        score_T = qk_sums[0:E, :, :]
        base = key[:, :, :].rearrange("p t e -> p (t e)").rearrange("p (t d) -> p t d", d=D)

        x_loaded = m.sems("x_loaded", 4)
        wr_loaded = m.sem("wr_loaded")
        weights_loaded = m.sem("weights_loaded")
        zero_made = m.sem("zero_made")
        zero_stored = m.sem("zero_stored")
        consts_made = m.sem("consts_made")
        stats_done = m.sem("stats_done")
        moments_done = m.sem("moments_done")
        pool_step = m.sem("pool_step")
        rstd_done = m.sem("rstd_done")
        xn_done = m.sem("xn_done")
        xt_ready = m.sem("xt_ready")
        xnT_done = m.sem("xnT_done")
        logits_done = m.sem("logits_done")
        sigmoid_done = m.sem("sigmoid_done")
        scores_turned = m.sem("scores_turned")
        score_done = m.sem("score_done")
        mask_done = m.sem("mask_done")
        counts_done = m.sem("counts_done")
        counts_read = m.sem("counts_read")
        index_done = m.sem("index_done")
        route_step = m.sem("route_step")
        staged = m.sem("staged")
        scattered = m.sems("scattered", 2)
        qk_ready = m.sem("qk_ready")
        qk_hi = m.sem("qk_hi")
        qk_lo = m.sem("qk_lo")
        qk_sum = m.sem("qk_sum")
        qk_stored = m.sems("qk_stored", 4)
        v_ready = m.sem("v_ready")
        v_summed = m.sem("v_summed")
        v_hi = m.sem("v_hi")
        v_lo = m.sem("v_lo")
        v_stored = m.sems("v_stored", 4)
        gu_ready = m.sem("gu_ready")
        silu_done = m.sem("silu_done")
        hid_done = m.sem("hid_done")
        down_ready = m.sem("down_ready")
        base_done = m.sem("base_done")
        base_stored = m.sem("base_stored")

        sp_waits, pool_waits = m.sem("sp_waits"), m.sem("pool_waits")
        block = stack.enter_context(nc.Block())
        XG = NT // 4
        ZR = SLOTS // P // 4
        N_WEIGHTS = 11
        ROUTED = 2
        ZEROS_FIRST = 10
        COUNTS_AT = 7

        def qk_units(c):
            for u in range(H):
                yield c * H + u, u, u % 2, u // 2

        @block.sync
        def _(sp):
            sp.dma_start(wr[:, :, :], io["wr"]).then_inc(wr_loaded, 16)
            for g in range(4):
                sp.dma_start(x_sb[:, g * XG:(g + 1) * XG, :],
                             io["x"][g * XG * P:(g + 1) * XG * P, :].rearrange("(t p) d -> p t d", p=P)
                             ).then_inc(x_loaded[g], 16)
            for dst, src in ((wq, io["wq"]), (wk, io["wk"]), (wv, io["wv"]), (wg, io["wg"]),
                             (wu, io["wu"]), (wd, io["wd"])):
                sp.dma_start(dst[:, :, :], src).then_inc(weights_loaded, 16)
            sp.dma_start(bq[:, :], io["bq"]).then_inc(weights_loaded, 16)
            sp.dma_start(bk[:, :], io["bk"]).then_inc(weights_loaded, 16)
            sp.dma_start(bv[:, :], io["bv"].partition_broadcast(P)).then_inc(weights_loaded, 16)
            sp.dma_start(bo[:, :], io["bo"].partition_broadcast(P)).then_inc(weights_loaded, 16)
            sp.dma_start(eb[:, :], io["eb"].partition_broadcast(P)).then_inc(weights_loaded, 16)
            sp.wait_ge(zero_made, 1)
            def zero_rows(g):
                sp.dma_start(scr["xbuf"].rearrange("(g p r) d -> g p (r d)", p=P, r=4)[g], zeros
                             ).then_inc(zero_stored, 16)

            for g in range(ZEROS_FIRST):
                zero_rows(g)
            sp.dma_start(scr["ye"][SLOTS:SLOTS + P, :], zeros[:, 0:D]).then_inc(zero_stored, 16)

            def store_qk(c):
                for n, u, is_key, pair in qk_units(c):
                    dst = scr["k" if is_key else "q"]
                    wait_apart(sp, qk_lo, n + 1, sp_waits)
                    for part, src in ((0, part_hi), (1, part_lo)):
                        sp.dma_start(dst[part, pair * P:(pair + 1) * P, bass.ds(c * CH, CH)],
                                     src[:, u % 4, :].bitcast(F32)).then_inc(qk_stored[u % 4], 16)
                    if isinstance(n, int) and n % 3 == 2:
                        zero_rows(ZEROS_FIRST + n // 3)

            for c in range(ROUTED):
                store_qk(c)
            for g in range(ZEROS_FIRST + ROUTED * H // 3, ZR):
                zero_rows(g)
            with sp.Fori(0, NC) as c:
                wait_apart(sp, base_done, c + 1, sp_waits)
                sp.dma_start(scr["base"][:, bass.ds(c * TPC, TPC), :], base[:, :, :]).then_inc(base_stored, 16)
            with sp.Fori(ROUTED, NC) as c:
                store_qk(c)
            for t in range(NT):
                for half in range(2):
                    n = 2 * t + half
                    wait_apart(sp, v_lo, n + 1, sp_waits)
                    sp.dma_start(scr["v"][half * 8:half * 8 + 8, :, t, :].rearrange("h p c -> p h c"),
                                 v_parts[n % 4].rearrange("p h a c -> p h (a c)").bitcast(F32)
                                 ).then_inc(v_stored[n % 4], 16)
            for q in range(2):
                sp.wait_ge(scattered[q], NT // 2 * K * 16)
            for e in range(2):
                load_expert(sp, io, scr, ahead, e, e)
            for n in range(4):
                sp.wait_ge(qk_stored[n], NC * H // 4 * 32)
            for n in range(4):
                sp.wait_ge(v_stored[n], 2 * NT // 4 * 16)
            sp.wait_ge(base_stored, NC * 16)
            sp.wait_ge(zero_stored, (ZR + 1) * 16)

        @block.gpsimd
        def _(pool):
            ident = keep["ident"]
            nc.gpsimd.memset(ident[:, :], 0.0)
            nc.gpsimd.memset(earlier[:, :], 1.0)
            nc.gpsimd.memset(onesb[:, :], 1.0)
            nc.gpsimd.memset(minus_half[:, :], -0.5).then_inc(pool_step, 1)
            pool.wait_ge(pool_step, 1)
            nc.gpsimd.affine_select(out=ident[:, :], in_=ident[:, :], compare_op=ALU.not_equal, fill=1.0,
                                    base=0, pattern=[[-1, P]], channel_multiplier=1)
            nc.gpsimd.affine_select(out=earlier[:, :], in_=earlier[:, :], compare_op=ALU.is_gt, fill=0.0,
                                    base=0, pattern=[[1, P]], channel_multiplier=-1)
            nc.gpsimd.iota(ebase[:, :, :], pattern=[[0, NT], [CAP, E]], base=1, channel_multiplier=0,
                           allow_small_or_imprecise_dtypes=True).then_inc(consts_made, 1)
            for g in range(4):
                tiles = slice(g * XG, (g + 1) * XG)
                wait_apart(pool, moments_done, g + 1, pool_waits)
                nc.gpsimd.tensor_scalar(veps[:, tiles], moments[:, tiles, 1], EPS, None, ALU.add
                                        ).then_inc(pool_step, 1)
                wait_apart(pool, pool_step, g + 2, pool_waits)
                nc.gpsimd.tensor_tensor(rstd[:, tiles], veps[:, tiles], minus_half[:, tiles], ALU.pow
                                        ).then_inc(rstd_done, 1)
            for c in range(ROUTED):
                for n, u, is_key, pair in qk_units(c):
                    pool.wait_ge(qk_sum, n + 1)
                    nc.gpsimd.tensor_tensor(part_lo[:, u % 4, :], qk_sums[:, u % 2, :],
                                            part_hi[:, u % 4, :].bitcast(F32), ALU.subtract).then_inc(qk_lo, 1)
            pool.wait_ge(index_done, 1)
            pool.wait_ge(zero_stored, (ZR + 1) * 16)

            def scatter(i):
                for q in range(2):
                    wait_apart(pool, scattered[q], i * (K * 16), pool_waits)
                    nc.gpsimd.tensor_copy(stage_i[:, q, :], keep["index"][:, bass.ds(2 * i + q, 1), :]
                                          .rearrange("p a k -> p (a k)"))
                    nc.gpsimd.tensor_copy(stage_x[:, q, :], xn[:, bass.ds(2 * i + q, 1), :]
                                          .rearrange("p a d -> p (a d)")).then_inc(staged, 1)
                    wait_apart(pool, staged, 2 * i + q + 1, pool_waits)
                    for k in range(K):
                        nc.gpsimd.indirect_dma_start(
                            out=scr["xbuf"][:, :],
                            out_offset=bass.IndirectOffsetOnAxis(ap=stage_i[:, q, k:k + 1], axis=0),
                            in_=stage_x[:, q, :], in_offset=None,
                            bounds_check=SLOTS - 1, oob_is_err=False).then_inc(scattered[q], 16)
            scatter(0)
            with pool.Fori(1, NT // 2) as i:
                scatter(i)
            for q in range(2):
                pool.wait_ge(scattered[q], NT // 2 * K * 16)

        @block.scalar
        def _(act):
            def sigmoid(c):
                act.wait_ge(logits_done, c + 1)
                wait_pos(act, scores_turned, c - 1)
                nc.scalar.activation(score_T[:, c % 2, :], ps[0:E, 6 + c % 2, :], ACT.Sigmoid
                                     ).then_inc(sigmoid_done, 1)

            for c in range(NC):
                for n in (2 * c, 2 * c + 1):
                    act.wait_ge(xt_ready, n + 1)
                    nc.scalar.copy(xnT[:, n % 2, c * CH:(c + 1) * CH], ps[:, n % 4, :]).then_inc(xnT_done, 1)
                if c:
                    sigmoid(c - 1)
            sigmoid(NC - 1)
            for half in range(2):
                act.wait_ge(scores_turned, (half + 1) * NC // 2)
                nc.scalar.copy(score[:, half * 16:half * 16 + 16, :],
                               ps[:, 4 + half, :].rearrange("p (t e) -> p t e", e=E)).then_inc(score_done, 1)

            def qk_high(c):
                for n, u, is_key, pair in qk_units(c):
                    bias = (bk if is_key else bq)[:, pair:pair + 1]
                    act.wait_ge(qk_ready, n + 1)
                    wait_pos(act, qk_stored[u % 4], (c * 4 + u // 4) * 32)
                    nc.scalar.activation(part_hi[:, u % 4, :], ps[:, 4 + u % 4, :], ACT.Identity, bias=bias
                                         ).then_inc(qk_hi, 1)
                    if isinstance(c, int):
                        wait_pos(act, qk_lo, n - 1)
                        nc.scalar.activation(qk_sums[:, u % 2, :], ps[:, 4 + u % 4, :], ACT.Identity, bias=bias
                                             ).then_inc(qk_sum, 1)

            for c in range(ROUTED):
                qk_high(c)
            with act.Fori(0, NC) as c:
                for u in range(4):
                    act.wait_ge(gu_ready, c * 4 + u + 1)
                    nc.scalar.activation(silu_g[:, u % 2, :], ps[:, 2 * (u % 2), :], ACT.Silu
                                         ).then_inc(silu_done, 1)
            with act.Fori(ROUTED, NC) as c:
                qk_high(c)
            for u in range(4):
                act.wait_ge(qk_stored[u], NC * H // 4 * 32)
            for n in range(2 * NT):
                act.wait_ge(v_summed, n + 1)
                wait_pos(act, v_stored[n % 4], (n // 4) * 16)
                nc.scalar.copy(v_parts[n % 4][:, :, 0, :],
                               v_sum[:, n % 2, :].rearrange("p (h c) -> p h c", c=DH)).then_inc(v_hi, 1)

        @block.vector
        def _(dve):
            nc.vector.memset(zeros, 0.0).then_inc(zero_made, 1)
            for g in range(4):
                tiles = range(g * XG, (g + 1) * XG)
                dve.wait_ge(x_loaded[g], 16)
                for t in tiles:
                    last = nc.vector.bn_stats(stats[:, t, :], x_sb[:, t, :])
                last.then_inc(stats_done, 1)
                dve.wait_ge(stats_done, g + 1)
                for t in tiles:
                    last = nc.vector.bn_aggr(moments[:, t, :], stats[:, t, :])
                last.then_inc(moments_done, 1)
                dve.wait_ge(moments_done, g + 1)
                dve.wait_ge(rstd_done, g + 1)
                for t in tiles:
                    last = nc.vector.tensor_scalar(xn[:, t, :], x_sb[:, t, :], moments[:, t, 0:1],
                                                   rstd[:, t:t + 1], ALU.subtract, ALU.mult)
                    if t % TPC == TPC - 1:
                        last.then_inc(xn_done, 1)

            steps = [0]

            def link(ins):
                steps[0] += 1
                ins.then_inc(route_step, 1)
                dve.wait_ge(route_step, steps[0])

            dve.wait_ge(xn_done, NC)
            dve.wait_ge(weights_loaded, N_WEIGHTS * 16)
            link(nc.vector.tensor_tensor(x_sb[:, :, :], x_sb[:, :, :],
                                         bo[:, :].unsqueeze(1).to_broadcast([P, NT, D]), ALU.add))
            dve.wait_ge(score_done, 2)
            link(nc.vector.tensor_tensor(key[:, :, :], score[:, :, :],
                                         eb[:, :].unsqueeze(1).to_broadcast([P, NT, E]), ALU.add))
            for t in range(NT):
                last = nc.vector.max(top[:, t, :], key[:, t, :])
            link(last)
            for t in range(NT):
                last = nc.vector.match_replace(ta[:, t, :], top[:, t, :], key[:, t, :], -3.0e38)
            link(last)
            nc.vector.tensor_tensor(maskb[:, :].rearrange("p (t e) -> p t e", e=E), ta[:, :, :], key[:, :, :],
                                    ALU.not_equal).then_inc(mask_done, 1)
            link(nc.vector.tensor_tensor(mask[:, :, :], ta[:, :, :], key[:, :, :], ALU.not_equal))
            link(nc.vector.tensor_tensor(weight[:, :, :], score[:, :, :], mask[:, :, :], ALU.mult))
            link(nc.vector.tensor_reduce(wsum[:, :], weight[:, :, :], AX.X, ALU.add))
            link(nc.vector.tensor_scalar(wsum[:, :], wsum[:, :], 1e-20, None, ALU.add))
            link(nc.vector.reciprocal(wsum[:, :], wsum[:, :]))
            link(nc.vector.tensor_tensor(weight[:, :, :], weight[:, :, :],
                                         wsum[:, :].unsqueeze(2).to_broadcast([P, NT, E]), ALU.mult))
            nc.vector.tensor_scalar(weight[:, :, :], weight[:, :, :], SCALE, None, ALU.mult)
            dve.wait_ge(counts_done, 1)
            counts = ps[:, 2:4, :].rearrange("p b (t e) -> p (b t) e", e=E)
            within = ps[:, 0:2, :].rearrange("p b (t e) -> p (b t) e", e=E)
            link(nc.vector.tensor_copy(ta[:, :, :], counts))
            a, b = ta, tb
            for s in (1, 2, 4, 8, 16):
                nc.vector.tensor_copy(b[:, 0:s, :], a[:, 0:s, :])
                link(nc.vector.tensor_tensor(b[:, s:NT, :], a[:, s:NT, :], a[:, 0:NT - s, :], ALU.add))
                a, b = b, a
            link(nc.vector.tensor_tensor(b[:, :, :], counts, a[:, :, :], ALU.subtract))
            nc.vector.tensor_tensor(a[:, :, :], within, b[:, :, :], ALU.subtract).then_inc(counts_read, 1)
            dve.wait_ge(counts_read, 1)
            link(nc.vector.scalar_tensor_tensor(out=b[:, :, :], in0=a[:, :, :], scalar=float(CAP),
                                                in1=mask[:, :, :], op0=ALU.is_lt, op1=ALU.mult))
            dve.wait_ge(consts_made, 1)
            link(nc.vector.tensor_tensor(a[:, :, :], a[:, :, :], ebase[:, :, :], ALU.add))
            link(nc.vector.tensor_tensor(key[:, :, :], a[:, :, :], b[:, :, :], ALU.mult))
            for t in range(NT):
                last = nc.vector.max(top[:, t, :], key[:, t, :])
            link(last)
            rows = ta[:, 0:K, :].rearrange("p k e -> p (k e)")
            flat = top[:, :, :].rearrange("p t k -> p (t k)")
            link(nc.vector.tensor_scalar(rows, flat, 0.0, float(SLOTS + 1), ALU.is_equal, ALU.mult))
            nc.vector.scalar_tensor_tensor(out=keep["index"][:, :, :].rearrange("p t k -> p (t k)"), in0=rows,
                                           scalar=-1.0, in1=flat, op0=ALU.add, op1=ALU.add
                                           ).then_inc(index_done, 1)
            dve.wait_ge(index_done, 1)
            for k in range(K):
                link(nc.vector.tensor_tensor(ta[:, :, :], key[:, :, :],
                                             top[:, :, k:k + 1].to_broadcast([P, NT, E]), ALU.is_equal))
                link(nc.vector.tensor_tensor(tb[:, :, :], ta[:, :, :], weight[:, :, :], ALU.mult))
                nc.vector.tensor_reduce(keep["gain"][:, :, k:k + 1], tb[:, :, :], AX.X, ALU.add)

            def shared(c):
                for u in range(4):
                    dve.wait_ge(silu_done, c * 4 + u + 1)
                    if u == 0:
                        wait_pos(dve, down_ready, c)
                    nc.vector.tensor_tensor(hid[:, u, :], silu_g[:, u % 2, :], ps[:, 2 * (u % 2) + 1, :],
                                            ALU.mult).then_inc(hid_done, 1)
                dve.wait_ge(down_ready, c + 1)
                wait_pos(dve, base_stored, c * 16)
                for h in range(2):
                    last = nc.vector.tensor_tensor(base[:, 2 * h:2 * h + 2, :],
                                                   ps[:, 4 + h, :].rearrange("p (t d) -> p t d", d=D),
                                                   x_sb[:, bass.ds(c * TPC + 2 * h, 2), :], ALU.add)
                last.then_inc(base_done, 1)

            shared(0)
            with dve.Fori(1, NC) as c:
                shared(c)

            dve.wait_ge(qk_lo, ROUTED * H)
            with dve.Fori(ROUTED, NC) as c:
                for n, u, is_key, pair in qk_units(c):
                    bias = (bk if is_key else bq)[:, pair:pair + 1]
                    dve.wait_ge(qk_hi, n + 1)
                    nc.vector.scalar_tensor_tensor(out=part_lo[:, u % 4, :], in0=ps[:, 4 + u % 4, :], scalar=bias,
                                                   in1=part_hi[:, u % 4, :].bitcast(F32), op0=ALU.add,
                                                   op1=ALU.subtract).then_inc(qk_lo, 1)

            def v_low(n):
                dve.wait_ge(v_hi, n + 1)
                nc.vector.tensor_tensor(v_parts[n % 4][:, :, 1, :],
                                        v_sum[:, n % 2, :].rearrange("p (h c) -> p h c", c=DH),
                                        v_parts[n % 4][:, :, 0, :].bitcast(F32), ALU.subtract).then_inc(v_lo, 1)

            dve.wait_ge(zero_stored, (ZR + 1) * 16)
            for n in range(2 * NT):
                dve.wait_ge(v_ready, n + 1)
                wait_pos(dve, v_lo, n - 1)
                nc.vector.tensor_tensor(v_sum[:, n % 2, :], ps[:, n % 4, :],
                                        bv[:, (n % 2) * 512:(n % 2 + 1) * 512], ALU.add).then_inc(v_summed, 1)
                if n:
                    v_low(n - 1)
            v_low(2 * NT - 1)


        @block.tensor
        def _(pe):
            def logits(c):
                pe.wait_ge(xnT_done, 2 * c + 2)
                wait_pos(pe, sigmoid_done, c - 1)
                for k in range(DK):
                    last = nc.tensor.matmul(ps[0:E, 6 + c % 2, :], wr[:, k, :], xnT[:, k, c * CH:(c + 1) * CH],
                                            start=(k == 0), stop=(k == DK - 1))
                last.then_inc(logits_done, 1)

            def turn_scores(c):
                pe.wait_ge(sigmoid_done, c + 1)
                for t in range(c * TPC, (c + 1) * TPC):
                    last = nc.tensor.transpose(ps[:, 4 + t // 16, (t % 16) * E:(t % 16 + 1) * E],
                                               score_T[:, c % 2, t % TPC * P:(t % TPC + 1) * P],
                                               keep["ident"][0:E, 0:E])
                last.then_inc(scores_turned, 1)

            pe.wait_ge(consts_made, 1)
            for c in range(NC):
                pe.wait_ge(xn_done, c + 1)
                for k in range(DK):
                    n = 2 * c + k
                    wait_pos(pe, xnT_done, n - 3)
                    for j in range(TPC):
                        last = nc.tensor.transpose(ps[:, n % 4, j * P:(j + 1) * P],
                                                   xn[:, c * TPC + j, k * P:(k + 1) * P], keep["ident"][:, :])
                    last.then_inc(xt_ready, 1)
                if c == 0:
                    pe.wait_ge(wr_loaded, 16)
                if c:
                    logits(c - 1)
                if c > 1:
                    turn_scores(c - 2)
            logits(NC - 1)
            turn_scores(NC - 2)
            turn_scores(NC - 1)

            def counts():
                pe.wait_ge(mask_done, 1)
                for h in range(2):
                    nc.tensor.matmul(ps[:, h, :], earlier[:, :], maskb[:, h * 512:(h + 1) * 512],
                                     start=True, stop=True)
                    last = nc.tensor.matmul(ps[:, 2 + h, :], onesb[:, :], maskb[:, h * 512:(h + 1) * 512],
                                            start=True, stop=True)
                last.then_inc(counts_done, 1)

            pe.wait_ge(weights_loaded, N_WEIGHTS * 16)
            pe.wait_ge(score_done, 2)
            def qk(c):
                for n, u, is_key, pair in qk_units(c):
                    w = wk if is_key else wq
                    wait_pos(pe, qk_lo, n - 3)
                    for k in range(DK):
                        last = nc.tensor.matmul(ps[:, 4 + u % 4, :], w[:, k, pair * P:(pair + 1) * P],
                                                xnT[:, k, bass.ds(c * CH, CH)],
                                                start=(k == 0), stop=(k == DK - 1))
                    last.then_inc(qk_ready, 1)
                    if isinstance(c, int) and n == COUNTS_AT:
                        counts()

            def gate_up(c, u):
                wait_pos(pe, hid_done, c * 4 + u - 1)
                for bank, w in ((2 * (u % 2), wg), (2 * (u % 2) + 1, wu)):
                    for k in range(DK):
                        last = nc.tensor.matmul(ps[:, bank, :], w[:, k, u * P:(u + 1) * P],
                                                xnT[:, k, bass.ds(c * CH, CH)],
                                                start=(k == 0), stop=(k == DK - 1))
                last.then_inc(gu_ready, 1)

            def shared(c, following):
                for u in range(1, 4):
                    gate_up(c, u)
                if following:
                    gate_up(c + 1, 0)
                pe.wait_ge(hid_done, c * 4 + 4)
                wait_pos(pe, base_done, c)
                for j in range(TPC):
                    for u in range(4):
                        last = nc.tensor.matmul(ps[:, 4 + j // 2, (j % 2) * D:(j % 2 + 1) * D],
                                                hid[:, u, j * P:(j + 1) * P], wd[:, u, :],
                                                start=(u == 0), stop=(u == 3))
                last.then_inc(down_ready, 1)

            for c in range(ROUTED):
                qk(c)
            pe.wait_ge(counts_read, 1)
            gate_up(0, 0)
            pe.wait_ge(qk_lo, ROUTED * H)
            shared(0, True)
            with pe.Fori(1, NC - 1) as c:
                shared(c, True)
            shared(NC - 1, False)
            pe.wait_ge(base_done, NC)
            with pe.Fori(ROUTED, NC) as c:
                qk(c)
            for n in range(2 * NT):
                t, half = n // 2, n % 2
                wait_pos(pe, v_summed, n - 3)
                for k in range(DK):
                    last = nc.tensor.matmul(ps[:, n % 4, :], xnT[:, k, t * P:(t + 1) * P],
                                            wv[:, k, half * 512:(half + 1) * 512],
                                            start=(k == 0), stop=(k == DK - 1))
                last.then_inc(v_ready, 1)




def load_expert(sp, io, scr, ahead, e, q):
    sp.dma_start(ahead["xe"][:, q, :, :], scr["xbuf"][bass.ds(e * CAP, CAP), :]
                 .rearrange("(t p) d -> p t d", p=P)).then_inc(ahead["loaded"][q], 16)
    sp.dma_start(ahead["gu"][:, q, :, :], io["gu"][bass.ds(e, 1), :, :, :]
                 .rearrange("a p k o -> p (a k) o")).then_inc(ahead["loaded"][q], 16)
    sp.dma_start(ahead["dn"][:, q, :], io["dn"][bass.ds(e, 1), :, :]
                 .rearrange("a p d -> p (a d)")).then_inc(ahead["loaded"][q], 16)


def run_experts(nc, io, scr, keep, ahead, start):
    with ExitStack() as stack:
        m = Memory(nc, stack, "ex")
        ps = m.ps("ps", [P, 8, CH])
        CT = CAP // P
        xe, gu, dn, loaded = (ahead[name] for name in ("xe", "gu", "dn", "loaded"))
        xeT = m.sb("xeT", [P, 2, DK, CAP])
        gate = m.sb("gate", [P, 2, CAP])
        up = m.sb("up", [P, 2, CAP])
        silu_g = m.sb("silu_g", [P, 2, CAP])
        hid = m.sb("hid", [P, 2, CAP])
        dn_old = m.sb("dn_old", [P, 2, D])
        ye = m.sb("ye", [P, 2, CT, D])

        turned = m.sem("turned")
        xeT_done = m.sem("xeT_done")
        gu_ready = m.sem("gu_ready")
        gate_done = m.sem("gate_done")
        up_done = m.sem("up_done")
        silu_done = m.sem("silu_done")
        hid_done = m.sem("hid_done")
        dn_kept = m.sem("dn_kept")
        down_ready = m.sem("down_ready")
        ye_done = m.sem("ye_done")
        stored = m.sems("stored", 2)
        sp_waits, pool_waits = m.sem("sp_waits"), m.sem("pool_waits")
        block = stack.enter_context(nc.Block())

        @block.sync
        def _(sp):
            def load(i):
                for q in range(2):
                    e = 2 * i + q
                    wait_apart(sp, turned, 2 * i + q - 1, sp_waits)
                    wait_apart(sp, gu_ready, 2 * i + q - 1, sp_waits)
                    wait_apart(sp, dn_kept, 2 * i + q - 1, sp_waits)
                    load_expert(sp, io, scr, ahead, e, q)

            load_k(sp, scr, start, 0, 0, 0)
            load_q(sp, scr, start, 0, 0, 0)
            with sp.Fori(1, E // 2) as i:
                load(i)

        @block.gpsimd
        def _(pool):
            def store(i):
                for q in range(2):
                    e = 2 * i + q
                    wait_apart(pool, ye_done, 2 * i + q + 1, pool_waits)
                    pool.dma_start(scr["ye"][bass.ds(e * CAP, CAP), :].rearrange("(t p) d -> p t d", p=P),
                                   ye[:, q, :, :]).then_inc(stored[q], 16)

            with pool.Fori(0, E // 2) as i:
                store(i)
            for q in range(2):
                pool.wait_ge(stored[q], E // 2 * 16)

        @block.scalar
        def _(act):
            def turn(i, q):
                n = 2 * i + q
                act.wait_ge(turned, n + 1)
                nc.scalar.copy(xeT[:, q, :, :], ps[:, 0:2, :]).then_inc(xeT_done, 1)

            def down(i, q):
                n = 2 * i + q
                act.wait_ge(down_ready, n + 1)
                wait_pos(act, stored[q], i * 16)
                nc.scalar.copy(ye[:, q, :, :].rearrange("p t d -> p (t d)"),
                               ps[:, 2:4, :].rearrange("p b c -> p (b c)")).then_inc(ye_done, 1)

            def silu(i, q):
                n = 2 * i + q
                act.wait_ge(gate_done, n + 1)
                nc.scalar.activation(silu_g[:, q, :], gate[:, q, :], ACT.Silu).then_inc(silu_done, 1)

            for q in range(2):
                turn(0, q)
                silu(0, q)

            def both(i):
                for q in range(2):
                    turn(i, q)
                    down(i - 1, q)
                    silu(i, q)

            both(1)
            with act.Fori(2, E // 2) as i:
                both(i)
            for q in range(2):
                down(E // 2 - 1, q)

        @block.vector
        def _(dve):
            def hidden(i):
                for q in range(2):
                    n = 2 * i + q
                    dve.wait_ge(gu_ready, n + 1)
                    wait_pos(dve, down_ready, n - 1)
                    nc.vector.tensor_copy(dn_old[:, q, :], dn[:, q, :]).then_inc(dn_kept, 1)
                    nc.vector.tensor_scalar(gate[:, q, :], ps[:, 4 + 2 * q, :], LIMIT, None, ALU.min
                                            ).then_inc(gate_done, 1)
                    nc.vector.tensor_scalar(up[:, q, :], ps[:, 5 + 2 * q, :], LIMIT, -LIMIT, ALU.min, ALU.max
                                            ).then_inc(up_done, 1)
                    dve.wait_ge(up_done, n + 1)
                    dve.wait_ge(silu_done, n + 1)
                    nc.vector.tensor_tensor(hid[:, q, :], silu_g[:, q, :], up[:, q, :], ALU.mult
                                            ).then_inc(hid_done, 1)

            hidden(0)
            with dve.Fori(1, E // 2) as i:
                hidden(i)

        @block.tensor
        def _(pe):
            def turn(i, q):
                pe.wait_ge(loaded[q], i * 48 + 48)
                wait_pos(pe, xeT_done, 2 * i + q)
                for k in range(DK):
                    for t in range(CT):
                        last = nc.tensor.transpose(ps[:, k, t * P:(t + 1) * P],
                                                   xe[:, q, t, k * P:(k + 1) * P], keep["ident"][:, :])
                last.then_inc(turned, 1)

            def gate_up(i, q):
                n = 2 * i + q
                pe.wait_ge(xeT_done, n + 1)
                wait_pos(pe, up_done, n - 1)
                for side in range(2):
                    for k in range(DK):
                        last = nc.tensor.matmul(ps[:, 4 + 2 * q + side, :], gu[:, q, k, side * I:(side + 1) * I],
                                                xeT[:, q, k, :], start=(k == 0), stop=(k == DK - 1))
                last.then_inc(gu_ready, 1)

            def down(i, q):
                n = 2 * i + q
                pe.wait_ge(hid_done, n + 1)
                pe.wait_ge(dn_kept, n + 1)
                wait_pos(pe, ye_done, n)
                for t in range(CT):
                    last = nc.tensor.matmul(ps[:, 2 + t // 2, (t % 2) * D:(t % 2 + 1) * D],
                                            hid[:, q, t * P:(t + 1) * P], dn_old[:, q, :], start=True, stop=True)
                last.then_inc(down_ready, 1)

            for q in range(2):
                turn(0, q)
                gate_up(0, q)
            def both(i):
                for q in range(2):
                    turn(i, q)
                    down(i - 1, q)
                    gate_up(i, q)

            both(1)
            with pe.Fori(2, E // 2) as i:
                both(i)
            for q in range(2):
                down(E // 2 - 1, q)



GT = 4
TILES = T // P
GROUPS = TILES // GT
PV_LAG = GT + 1
OUT_LAG = 2 * GT + 1
LAST = OUT_LAG + TILES
BANK = (4, 5, 7, 7)
FREED = (4, 4, 3, 1)
OUT_BANK = 4
BACK = (1, 1, 1, 2)


def load_q(sp, scr, start, b, h, g):
    for part, dst in ((0, start["q_hh"]), (1, start["q_ll"])):
        src = scr["q"][part, bass.ds(h * DH, DH), b * T + g * CH:b * T + (g + 1) * CH]
        for rows_ in (slice(0, DH), slice(DH, P)):
            sp.dma_start(dst[rows_, g % 2, :].bitcast(F32), src).then_inc(start["q_loaded"][g % 2], 16)


def load_k(sp, scr, start, b, h, side):
    for part in range(2):
        sp.dma_start(start["k_hl"][part * DH:(part + 1) * DH, side, :].bitcast(F32),
                     scr["k"][part, bass.ds(h * DH, DH), b * T:(b + 1) * T]).then_inc(start["k_loaded"][side], 16)


def attend(nc, io, scr, keep, ahead, start):
    with ExitStack() as stack:
        m = Memory(nc, stack, "at")
        ps = m.ps("ps", [P, 8, CH])
        q_hh, q_ll, k_hl, q_loaded, k_loaded = (start[name] for name in ("q_hh", "q_ll", "k_hl",
                                                                         "q_loaded", "k_loaded"))
        v_hl = m.sb("v_hl", [P, NS, P], F32R)
        wo = ahead["dn"]
        oT = ahead["xe"][:, 0, :, :].rearrange("p t d -> p (t d)").rearrange("p (g c) -> p g c", c=CH)
        acc_last = ahead["xe"][:, 1, :, :]
        prob = m.sb("prob", [P, 2, T])
        pT_hi = m.sb("pT_hi", [P, 2, NS, CH], F32R)
        pT_lo = m.sb("pT_lo", [P, 2, NS, CH], F32R)
        acc_first = m.sb("acc", [P, TILES - CAP // P, D])
        half_max = m.sb("half_max", [P, 2, 2])
        neg_max = m.sb("neg_max", [P, 2])
        half_sum = m.sb("half_sum", [P, TILES, 2])
        total = m.sb("total", [P, TILES])
        inv = m.sb("inv", [P, TILES])

        g_index = m.sb("g_index", [P, K], U32)
        g_gain = m.sb("g_gain", [P, K])
        rows = ahead["gu"][:, :, :, :].rearrange("p q k o -> p (q k) o")
        rest = m.sb("rest", [P, D])
        rest_t = rows[:, 0:2, :]

        v_loaded = m.sems("v_loaded", GT)
        wo_loaded = m.sems("wo_loaded", 2)
        scored = m.sem("scored")
        max_step = m.sem("max_step")
        max_done = m.sem("max_done")
        exp_done = m.sem("exp_done")
        turned = m.sem("turned")
        high_done = m.sem("high_done")
        low_done = m.sem("low_done")
        pv_done = m.sem("pv_done")
        oT_done = m.sem("oT_done")
        sum_step = m.sem("sum_step")
        inv_done = m.sem("inv_done")
        projected = m.sem("projected")
        cleared = m.sem("cleared")
        added = m.sem("added")
        rest_loaded = m.sems("rest_loaded", 2)
        finished = m.sem("finished")
        stored = m.sem("stored")
        restarted = m.sem("restarted")
        out_stored = m.sem("out_stored")
        g_staged = m.sem("g_staged")
        g_base = m.sem("g_base")
        gathered = m.sem("gathered")
        g_step = m.sem("g_step")
        g_stored = m.sem("g_stored")
        sp_waits, pool_waits = m.sem("sp_waits"), m.sem("pool_waits")
        block = stack.enter_context(nc.Block())

        def acc(t):
            return acc_first[:, t, :] if t < TILES - CAP // P else acc_last[:, t - (TILES - CAP // P), :]

        def slots(b, h):
            head = b * H + h
            opens = b == 0 and isinstance(h, int) and h == 0
            for s in range(LAST if b == B - 1 and isinstance(h, int) and h == H - 1 else TILES):
                tile = head * TILES + s
                back = [(s - 1) // GT, (s - PV_LAG) // GT, (s - OUT_LAG) // GT]
                turn = not opens or s >= 1
                late = not opens or s >= 2
                pv = not opens or s >= PV_LAG
                out = not opens or s >= OUT_LAG
                yield dict(
                    s=s, head=head, tile=tile, scores=s < TILES, turn=turn and s <= TILES,
                    late=late and s <= TILES + 1,
                    pv=(head * GROUPS + back[1], back[1] % 2, (s - PV_LAG) % GT)
                    if pv and s < PV_LAG + TILES else None,
                    out=(head * GROUPS + back[2], back[2] % GROUPS, (s - OUT_LAG) % GT, s < OUT_LAG)
                    if out and s < OUT_LAG + TILES else None)

        def over_heads(eng, body):
            for b in range(B):
                for s in slots(b, 0):
                    body(b, 0, s)
                with eng.Fori(1, H - 1) as h:
                    for s in slots(b, h):
                        body(b, h, s)
                for s in slots(b, H - 1):
                    body(b, H - 1, s)

        @block.sync
        def _(sp):
            def next_q(b, h, g):
                group = (b * H + h) * GROUPS + g
                wait_apart(sp, scored, 2 * GT * (group - 1), sp_waits)
                load_q(sp, scr, start, b, h, g)

            def next_k(b, h, side):
                head = b * H + h
                wait_apart(sp, scored, 2 * ((head - 1) * TILES + (side + 1) * TILES // 2), sp_waits)
                load_k(sp, scr, start, b, h, side)

            def load_v(b, h, quarter):
                wait_apart(sp, pv_done, GT * ((b * H + h) * GROUPS - 1) + quarter + 1, sp_waits)
                tiles = slice(quarter * GT, (quarter + 1) * GT)
                sp.dma_start(v_hl[:, tiles, :].bitcast(F32),
                             scr["v"][bass.ds(h, 1), :, b * NS + quarter * GT:b * NS + (quarter + 1) * GT, :]
                             .rearrange("a p t c -> p (a t) c")).then_inc(v_loaded[quarter], 16)

            def load_wo(b, h, side):
                wait_apart(sp, projected, (b * H + h) * TILES - TILES // 2 * (1 - side), sp_waits)
                sp.dma_start(wo[:, side, :], io["wo"][bass.ds(h, 1), :, :].rearrange("a p d -> p (a d)")
                             ).then_inc(wo_loaded[side], 16)

            def head_loads(b, h, following):
                next_q(b, h, 1)
                next_k(b, h, 1)
                load_wo(b, h, 0)
                for quarter in range(GT):
                    load_v(b, h, quarter)
                next_q(b, h, 2)
                next_q(b, h, 3)
                load_wo(b, h, 1)
                if following is not None:
                    next_k(*following, 0)
                    next_q(*following, 0)

            for b in range(B):
                head_loads(b, 0, (b, 1))
                with sp.Fori(1, H - 1) as h:
                    head_loads(b, h, (b, h + 1))
                head_loads(b, H - 1, (b + 1, 0) if b + 1 < B else None)
            for t in range(TILES):
                sp.wait_ge(added, (B * H - 1) * TILES + t + 1)
                sp.dma_start(io["out"][(NT - TILES + t) * P:(NT - TILES + t + 1) * P, :], acc(t)
                             ).then_inc(out_stored, 16)
            sp.wait_ge(out_stored, TILES * 16)

        @block.gpsimd
        def _(pool):
            def gather(n, k):
                nc.gpsimd.indirect_dma_start(
                    out=rows[:, k % 4, :], out_offset=None, in_=scr["ye"][:, :],
                    in_offset=bass.IndirectOffsetOnAxis(ap=g_index[:, k:k + 1], axis=0),
                    bounds_check=SLOTS, oob_is_err=True).then_inc(gathered, 16)

            with pool.Fori(0, NT) as n:
                nc.gpsimd.tensor_copy(g_index[:, :], keep["index"][:, bass.ds(n, 1), :]
                                      .rearrange("p a k -> p (a k)"))
                nc.gpsimd.tensor_copy(g_gain[:, :], keep["gain"][:, bass.ds(n, 1), :]
                                      .rearrange("p a k -> p (a k)")).then_inc(g_staged, 1)
                pool.dma_start(rest[:, :], scr["base"][:, bass.ds(n, 1), :].rearrange("p a d -> p (a d)")
                               ).then_inc(g_base, 16)
                wait_apart(pool, g_staged, n + 1, pool_waits)
                for r in range(2):
                    for k in range(4 * r, 4 * r + 4):
                        gather(n, k)
                    if r == 0:
                        wait_apart(pool, g_base, n * 16 + 16, pool_waits)
                    wait_apart(pool, gathered, n * (K * 16) + (r + 1) * 64, pool_waits)
                    for k in range(4):
                        nc.gpsimd.tensor_scalar(rows[:, k, :], rows[:, k, :], g_gain[:, 4 * r + k:4 * r + k + 1],
                                                None, ALU.mult).then_inc(g_step, 1)
                        wait_apart(pool, g_step, n * (2 * K) + 8 * r + 2 * k + 1, pool_waits)
                        nc.gpsimd.tensor_tensor(rest[:, :], rest[:, :], rows[:, k, :], ALU.add).then_inc(g_step, 1)
                        wait_apart(pool, g_step, n * (2 * K) + 8 * r + 2 * k + 2, pool_waits)
                pool.dma_start(scr["rest"][:, bass.ds(n, 1), :].rearrange("p a d -> p (a d)"), rest[:, :]
                               ).then_inc(g_stored, 16)
                wait_apart(pool, g_stored, n * 16 + 16, pool_waits)
            for t in range(2):
                pool.dma_start(rest_t[:, t, :], scr["rest"][:, t, :]).then_inc(rest_loaded[t], 16)
            for t in range(TILES):
                pool.wait_ge(finished, t + 1)
                pool.dma_start(io["out"][t * P:(t + 1) * P, :], acc(t)).then_inc(stored, 16)
                if t + 2 < TILES:
                    pool.dma_start(rest_t[:, t % 2, :], scr["rest"][:, t + 2, :]).then_inc(rest_loaded[t % 2], 16)
                pool.wait_ge(stored, 16 * (t + 1))
                pool.dma_start(acc(t), scr["rest"][:, TILES + t, :]).then_inc(restarted, 16)

        @block.tensor
        def _(pe):
            def transpose(s, unit):
                n = (s["tile"] - BACK[unit]) * GT + unit
                if unit % 2 == 0:
                    pe.wait_ge(exp_done, 2 * s["tile"] - 1 + unit // 2)
                wait_pos(pe, low_done, n + 1 - FREED[unit])
                if BANK[unit] == OUT_BANK and s["out"]:
                    wait_pos(pe, added, s["out"][0] * GT + s["out"][2])
                for j in range(GT):
                    t = unit * GT + j
                    last = nc.tensor.transpose(ps[:, BANK[unit], j * P:(j + 1) * P],
                                               prob[:, (s["s"] - BACK[unit]) % 2, t * P:(t + 1) * P], keep["ident"][:, :])
                last.then_inc(turned, 1)

            def score(s, half):
                i, head = s["s"], s["head"]
                g, j, side = i // GT, i % GT, i // (TILES // 2)
                if half == 0 and j == 0:
                    pe.wait_ge(q_loaded[g % 2], 64 * (head * 2 + g // 2) + 64)
                if half == 0 and i % (TILES // 2) == 0:
                    pe.wait_ge(k_loaded[side], 32 * head + 32)
                wait_pos(pe, exp_done, 2 * s["tile"] - 1 + half)
                for c in (2 * half, 2 * half + 1):
                    for q, first in ((q_hh, True), (q_ll, False)):
                        last = nc.tensor.matmul(ps[:, c, :], q[:, g % 2, j * P:(j + 1) * P],
                                                k_hl[:, side, c * CH:(c + 1) * CH],
                                                start=first, stop=not first)
                last.then_inc(scored, 1)

            def times_v(s):
                group, parity, quarter = s["pv"]
                pe.wait_ge(low_done, group * (GT * GT) + (GT - 1) * GT + quarter + 1)
                pe.wait_ge(v_loaded[quarter],
                           16 * (s["head"] + (1 if s["s"] >= PV_LAG else 0)))
                if quarter == 0:
                    wait_pos(pe, oT_done, group)
                for t in range(quarter * GT, (quarter + 1) * GT):
                    for part in (pT_hi, pT_lo):
                        last = nc.tensor.matmul(ps[:, 6, :], v_hl[:, t, :], part[:, parity, t, :],
                                                start=(t == 0 and part is pT_hi),
                                                stop=(t == NS - 1 and part is pT_lo))
                last.then_inc(pv_done, 1)

            def project(s):
                group, g, j, behind = s["out"]
                n = group * GT + j
                if j == 0:
                    pe.wait_ge(oT_done, group + 1)
                    pe.wait_ge(wo_loaded[g // 2], 16 * (s["head"] + (0 if behind else 1)))
                wait_pos(pe, added, n)
                if s["turn"]:
                    pe.wait_ge(low_done, (s["tile"] - 1) * GT + 1)
                nc.tensor.matmul(ps[:, OUT_BANK, 0:D], oT[:, g % 2, j * P:(j + 1) * P], wo[:, g // 2, :],
                                 start=True, stop=True).then_inc(projected, 1)

            def body(b, h, s):
                if s["scores"]:
                    score(s, 0)
                if s["late"]:
                    transpose(s, 3)
                if s["turn"]:
                    transpose(s, 0)
                if s["scores"]:
                    score(s, 1)
                if s["turn"]:
                    transpose(s, 1)
                    transpose(s, 2)
                if s["pv"]:
                    times_v(s)
                if s["out"]:
                    project(s)

            over_heads(pe, body)

        @block.scalar
        def _(act):
            def high(s, unit):
                i = s["s"] - BACK[unit]
                n = (s["tile"] - BACK[unit]) * GT + unit
                act.wait_ge(turned, n + 1)
                nc.scalar.copy(pT_hi[:, i // GT % 2, unit * GT:(unit + 1) * GT, i % GT * P:(i % GT + 1) * P],
                               ps[:, BANK[unit], :].rearrange("p (t c) -> p t c", c=P)).then_inc(high_done, 1)

            def exponent(s, half):
                i, tile = s["s"], s["tile"]
                if half == 0:
                    act.wait_ge(max_done, tile + 1)
                wait_pos(act, turned, GT * (tile - 2) + 2 * half + 2)
                nc.scalar.activation(prob[:, i % 2, half * 1024:(half + 1) * 1024],
                                     ps[:, 2 * half:2 * half + 2, :].rearrange("p b c -> p (b c)"),
                                     ACT.Exp, bias=neg_max[:, i % 2:i % 2 + 1], scale=DH ** -0.5,
                                     accum_out=half_sum[:, i % TILES, half:half + 1]).then_inc(exp_done, 1)

            def body(b, h, s):
                if s["late"]:
                    high(s, 3)
                if s["turn"]:
                    for unit in range(3):
                        high(s, unit)
                if s["scores"]:
                    exponent(s, 0)
                    exponent(s, 1)
                if s["pv"] and s["pv"][2] == GT - 1:
                    group, parity, _ = s["pv"]
                    act.wait_ge(pv_done, GT * (group + 1))
                    wait_pos(act, projected, GT * (group - 1))
                    nc.scalar.copy(oT[:, parity, :], ps[:, 6, :]).then_inc(oT_done, 1)

            over_heads(act, body)

        @block.vector
        def _(dve):
            def low(s, unit):
                i = s["s"] - BACK[unit]
                n = (s["tile"] - BACK[unit]) * GT + unit
                dve.wait_ge(high_done, n + 1)
                where = (slice(None), i // GT % 2, slice(unit * GT, (unit + 1) * GT), slice(i % GT * P, (i % GT + 1) * P))
                nc.vector.tensor_tensor(pT_lo[where], ps[:, BANK[unit], :].rearrange("p (t c) -> p t c", c=P),
                                        pT_hi[where].bitcast(F32), ALU.subtract).then_inc(low_done, 1)

            def maximum(s, half):
                i, tile = s["s"], s["tile"]
                dve.wait_ge(scored, 2 * tile + half + 1)
                nc.vector.tensor_reduce(half_max[:, i % 2, half:half + 1], ps[:, 2 * half:2 * half + 2, :],
                                        AX.XY, ALU.max).then_inc(max_step, 1)
                if half == 1:
                    dve.wait_ge(max_step, 2 * tile + 2)
                    wait_pos(dve, exp_done, 2 * (tile - 1))
                    nc.vector.tensor_scalar(neg_max[:, i % 2:i % 2 + 1], half_max[:, i % 2, 0:1],
                                            half_max[:, i % 2, 1:2], -(DH ** -0.5), ALU.max, ALU.mult
                                            ).then_inc(max_done, 1)

            def body(b, h, s):
                i, head = s["s"], s["head"]
                first = isinstance(h, int) and h == 0
                if first and b == 0 and i == 0:
                    nc.vector.memset(acc_first[:, :, :], 0.0)
                    nc.vector.memset(acc_last, 0.0).then_inc(cleared, 1)
                if s["scores"]:
                    maximum(s, 0)
                if s["late"]:
                    low(s, 3)
                if s["scores"]:
                    maximum(s, 1)
                if s["turn"]:
                    for unit in range(3):
                        low(s, unit)
                if s["out"]:
                    group, g, j, behind = s["out"]
                    n, t = group * GT + j, g * GT + j
                    dve.wait_ge(projected, n + 1)
                    if j == 0:
                        dve.wait_ge(inv_done, group + 1)
                    if first and b == 0 and i == OUT_LAG:
                        dve.wait_ge(cleared, 1)
                    if first and b == 1 and i >= OUT_LAG:
                        dve.wait_ge(restarted, 16 * (t + 1 if i < TILES - 1 else TILES))
                    wait_pos(dve, added, n - TILES // 2 + 1)
                    nc.vector.scalar_tensor_tensor(out=acc(t), in0=ps[:, OUT_BANK, 0:D], scalar=inv[:, t:t + 1],
                                                   in1=acc(t), op0=ALU.mult, op1=ALU.add
                                                   ).then_inc(added, 1)
                    if isinstance(head, int) and (head - behind + 1) == H:
                        dve.wait_ge(rest_loaded[t % 2], 16 * (t // 2 + 1))
                        dve.wait_ge(added, n + 1)
                        nc.vector.tensor_tensor(acc(t), acc(t), rest_t[:, t % 2, :], ALU.add
                                                ).then_inc(finished, 1)
                if s["pv"] and s["pv"][2] == 0:
                    group = s["pv"][0]
                    g = (s["s"] - PV_LAG) // GT % GROUPS
                    tiles = slice(g * GT, (g + 1) * GT)
                    dve.wait_ge(exp_done, 2 * GT * (group + 1))
                    nc.vector.tensor_tensor(total[:, tiles], half_sum[:, tiles, 0], half_sum[:, tiles, 1], ALU.add
                                            ).then_inc(sum_step, 1)
                    dve.wait_ge(sum_step, group + 1)
                    nc.vector.reciprocal(inv[:, tiles], total[:, tiles]).then_inc(inv_done, 1)

            over_heads(dve, body)


def build(nc, io):
    scr = {
        "xbuf": nc.dram_tensor("xbuf", (SLOTS, D), F32, kind="Internal").ap(),
        "ye": nc.dram_tensor("ye", (SLOTS + P, D), F32, kind="Internal").ap(),
        "q": nc.dram_tensor("q_parts", (2, H * DH, TOK), F32, kind="Internal").ap(),
        "k": nc.dram_tensor("k_parts", (2, H * DH, TOK), F32, kind="Internal").ap(),
        "v": nc.dram_tensor("v_parts", (H, P, NT, P), F32, kind="Internal").ap(),
        "base": nc.dram_tensor("base", (P, NT, D), F32, kind="Internal").ap(),
        "rest": nc.dram_tensor("rest", (P, NT, D), F32, kind="Internal").ap(),
    }
    with ExitStack() as stack:
        m = Memory(nc, stack, "keep")
        keep = {
            "ident": m.sb("ident", [P, P]),
            "index": m.sb("index", [P, NT, K], U32),
            "gain": m.sb("gain", [P, NT, K]),
        }
        with ExitStack() as across:
            n = Memory(nc, across, "ahead")
            ahead = {
                "xe": n.sb("xe", [P, 2, CAP // P, D]),
                "gu": n.sb("gu", [P, 2, DK, 2 * I]),
                "dn": n.sb("dn", [P, 2, D]),
                "loaded": n.sems("loaded", 2),
            }
            project_and_route(nc, io, scr, keep, ahead)
            start = {
                "q_hh": n.sb("q_hh", [P, 2, CH], F32R),
                "q_ll": n.sb("q_ll", [P, 2, CH], F32R),
                "k_hl": n.sb("k_hl", [P, 2, T], F32R),
                "q_loaded": n.sems("q_loaded", 2),
                "k_loaded": n.sems("k_loaded", 2),
            }
            run_experts(nc, io, scr, keep, ahead, start)
            attend(nc, io, scr, keep, ahead, start)


def kernel(**inputs):
    import numpy as np
    import concourse.bacc as bacc
    from concourse.bass_utils import run_bass_kernel_spmd

    a = {n: np.asarray(v) for n, v in inputs.items()}

    def halves(w):
        return w.T.reshape(DK, P, -1).transpose(1, 0, 2)

    wo = a["L0_attn_W_O"].transpose(0, 2, 1)
    gu = a["L0_ffn_gate_up_proj"].transpose(0, 2, 1).reshape(E, DK, P, 2 * I)
    laid = {
        "x": a["L0_attn_x"].reshape(TOK, D),
        "wq": halves(a["L0_attn_W_Q"].reshape(H * DH, D)),
        "wk": halves(a["L0_attn_W_K"].reshape(H * DH, D)),
        "wv": halves(a["L0_attn_W_V"].reshape(H * DH, D)),
        "bq": a["L0_attn_b_Q"].reshape(H // 2, P).T,
        "bk": a["L0_attn_b_K"].reshape(H // 2, P).T,
        "bv": a["L0_attn_b_V"].reshape(H * DH),
        "bo": a["L0_attn_b_O"],
        "wo": np.concatenate([wo, wo], axis=1),
        "wr": halves(a["L0_ffn_router_weight"]),
        "eb": a["L0_ffn_e_score_correction_bias"],
        "gu": gu.transpose(0, 2, 1, 3),
        "dn": a["L0_ffn_down_proj"].transpose(0, 2, 1),
        "wg": halves(a["L0_ffn_shared_gate"]),
        "wu": halves(a["L0_ffn_shared_up"]),
        "wd": a["L0_ffn_shared_down"].T.reshape(SI // P, P, D).transpose(1, 0, 2),
    }
    nc = bacc.Bacc("TRN2", target_bir_lowering=False, num_devices=1)
    arrays, io = {}, {}
    for name, v in laid.items():
        v = np.ascontiguousarray(v)
        arrays[f"in_{name}"] = v
        io[name] = nc.dram_tensor(f"in_{name}", v.shape, mybir.dt.from_np(v.dtype), kind="ExternalInput").ap()
    io["out"] = nc.dram_tensor("out", (TOK, D), F32, kind="ExternalOutput").ap()
    build(nc, io)
    r = run_bass_kernel_spmd(nc, [arrays], core_ids=[0])
    return r.results[0]["out"].reshape(B, T, D)
```
